# Optimizing a Trainium2 kernel written in Bass

```python
import numpy as np
import jax
import jax.numpy as jnp

def _softmax(x, axis=-1):
    return jax.nn.softmax(x, axis=axis)
def _gelu(x):
    return jax.nn.gelu(x, approximate=True)
def _silu(x):
    return jax.nn.silu(x)
def _sigmoid(x):
    return jax.nn.sigmoid(x)
def _layernorm(x, axis=-1, eps=1e-5):
    m = jnp.mean(x, axis=axis, keepdims=True)
    v = jnp.var(x, axis=axis, keepdims=True)
    return (x - m) / jnp.sqrt(v + eps)
def _scatter_add(tgt, idx, src, axis=0):
    return tgt.at[idx].add(src)
def _segment_sum(src, seg, n):
    return jax.ops.segment_sum(src, seg, n)

kernel_name = 'mk_conv_preact_d2_conv_nchw128_4916a9'

def setup_inputs(seed: int = 0):
    np.random.seed(seed)
    _w = jnp.asarray
    def _rec_inputs():
        import jax
        import jax.numpy as jnp
        _gk = jax.random.key(seed)
        x = -7.109e-05 + 0.9999 * jax.random.normal(jax.random.fold_in(_gk, 1), (8, 128, 256, 256), jnp.float32)
        return x
    x = _rec_inputs()
    def _L0_conv_setup():
        import jax, jax.numpy as jnp
        import numpy as np
        from jax import lax
        EPS = 1e-05

        def haar_dwt(x):
            B, C, H, W = x.shape
            xr = x.reshape(B, C, H // 2, 2, W // 2, 2)
            x00 = xr[:, :, :, 0, :, 0]
            x01 = xr[:, :, :, 0, :, 1]
            x10 = xr[:, :, :, 1, :, 0]
            x11 = xr[:, :, :, 1, :, 1]
            ll = (x00 + x01 + x10 + x11) * 0.5
            lh = (x00 + x01 - x10 - x11) * 0.5
            hl = (x00 - x01 + x10 - x11) * 0.5
            hh = (x00 - x01 - x10 + x11) * 0.5
            return (ll, lh, hl, hh)

        def haar_idwt(ll, lh, hl, hh):
            y00 = (ll + lh + hl + hh) * 0.5
            y01 = (ll + lh - hl - hh) * 0.5
            y10 = (ll - lh + hl - hh) * 0.5
            y11 = (ll - lh - hl + hh) * 0.5
            B, C, H, W = ll.shape
            top = jnp.stack([y00, y01], axis=-1)
            bot = jnp.stack([y10, y11], axis=-1)
            y = jnp.stack([top, bot], axis=3)
            return y.reshape(B, C, 2 * H, 2 * W)

        def conv1x1(x, w, b):
            return jnp.einsum('bchw,oc->bohw', x, w) + b[None, :, None, None]

        def batchnorm(x, g, b):
            mu = jnp.mean(x, axis=(0, 2, 3), keepdims=True)
            var = jnp.var(x, axis=(0, 2, 3), keepdims=True)
            xh = (x - mu) * lax.rsqrt(var + EPS)
            return xh * g[None, :, None, None] + b[None, :, None, None]

        def layernorm_chw(x, g, b):
            mu = jnp.mean(x, axis=(1, 2, 3), keepdims=True)
            var = jnp.var(x, axis=(1, 2, 3), keepdims=True)
            xh = (x - mu) * lax.rsqrt(var + EPS)
            return xh * g[None, :, None, None] + b[None, :, None, None]

        def dwconv3x3(x, w, b):
            C = x.shape[1]
            y = lax.conv_general_dilated(x, w, (1, 1), [(1, 1), (1, 1)], dimension_numbers=('NCHW', 'OIHW', 'NCHW'), feature_group_count=C)
            return y + b[None, :, None, None]
        gelu = lambda x: jax.nn.gelu(x, approximate=False)
        key = jax.random.key(seed)
        ks = jax.random.split(key, 16)
        C = 128
        B, H, W = (8, 256, 256)
        f = jnp.float32
        s = lambda k, shape, fan: jax.random.normal(k, shape, f) * (1.0 / np.sqrt(fan))
        return {'x': jax.random.normal(ks[0], (B, C, H, W), f), 'w_c1': s(ks[1], (C, 4 * C), 4 * C), 'b_c1': jnp.zeros((C,), f), 'bn1_g': jnp.ones((C,), f), 'bn1_b': jnp.zeros((C,), f), 'dw_w': s(ks[2], (C, 1, 3, 3), 9), 'dw_b': jnp.zeros((C,), f), 'gn_g': jnp.ones((C,), f), 'gn_b': jnp.zeros((C,), f), 'pw1_w': s(ks[3], (C, C), C), 'pw1_b': jnp.zeros((C,), f), 'pw2_w': s(ks[4], (C, C), C), 'pw2_b': jnp.zeros((C,), f), 'w_c2': s(ks[5], (4 * C, C), C), 'b_c2': jnp.zeros((4 * C,), f), 'bn2_g': jnp.ones((4 * C,), f), 'bn2_b': jnp.zeros((4 * C,), f)}
    _L0_conv_all = _L0_conv_setup()
    _L0_conv_in = {k: v for k, v in _L0_conv_all.items() if k in ('w_c1', 'b_c1', 'bn1_g', 'bn1_b', 'dw_w', 'dw_b', 'gn_g', 'gn_b', 'pw1_w', 'pw1_b', 'pw2_w', 'pw2_b', 'w_c2', 'b_c2', 'bn2_g', 'bn2_b', )}
    del _L0_conv_all

    def _L1_conv_setup():
        import jax, jax.numpy as jnp
        from jax import lax
        import numpy as np
        B, C, H, W = (8, 128, 256, 256)
        PAD0, PAD1 = (2, 1)
        UPSAMPLE_FACTOR = 2

        def _make_kernel():
            k1 = jnp.array([1.0, 3.0, 3.0, 1.0], dtype=jnp.float32)
            k = k1[:, None] * k1[None, :]
            k = k / jnp.sum(k)
            k = k * UPSAMPLE_FACTOR ** 2
            return k
        key = jax.random.key(seed)
        x = jax.random.normal(key, (B, C, H, W), dtype=jnp.float32)
        kernel = _make_kernel()
        return {'input': x, 'kernel': kernel}
    _L1_conv_all = _L1_conv_setup()
    _L1_conv_in = {k: v for k, v in _L1_conv_all.items() if k in ('kernel', )}
    del _L1_conv_all

    return {
        "x": x,
        "L0_conv_w_c1": _L0_conv_in["w_c1"],
        "L0_conv_b_c1": _L0_conv_in["b_c1"],
        "L0_conv_bn1_g": _L0_conv_in["bn1_g"],
        "L0_conv_bn1_b": _L0_conv_in["bn1_b"],
        "L0_conv_dw_w": _L0_conv_in["dw_w"],
        "L0_conv_dw_b": _L0_conv_in["dw_b"],
        "L0_conv_gn_g": _L0_conv_in["gn_g"],
        "L0_conv_gn_b": _L0_conv_in["gn_b"],
        "L0_conv_pw1_w": _L0_conv_in["pw1_w"],
        "L0_conv_pw1_b": _L0_conv_in["pw1_b"],
        "L0_conv_pw2_w": _L0_conv_in["pw2_w"],
        "L0_conv_pw2_b": _L0_conv_in["pw2_b"],
        "L0_conv_w_c2": _L0_conv_in["w_c2"],
        "L0_conv_b_c2": _L0_conv_in["b_c2"],
        "L0_conv_bn2_g": _L0_conv_in["bn2_g"],
        "L0_conv_bn2_b": _L0_conv_in["bn2_b"],
        "L1_conv_kernel": _L1_conv_in["kernel"],
    }

def reference(x, L0_conv_w_c1, L0_conv_b_c1, L0_conv_bn1_g, L0_conv_bn1_b, L0_conv_dw_w, L0_conv_dw_b, L0_conv_gn_g, L0_conv_gn_b, L0_conv_pw1_w, L0_conv_pw1_b, L0_conv_pw2_w, L0_conv_pw2_b, L0_conv_w_c2, L0_conv_b_c2, L0_conv_bn2_g, L0_conv_bn2_b, L1_conv_kernel):
    import jax
    import jax.numpy as jnp
    def _L0_conv_ref(x, w_c1, b_c1, bn1_g, bn1_b, dw_w, dw_b, gn_g, gn_b, pw1_w, pw1_b, pw2_w, pw2_b, w_c2, b_c2, bn2_g, bn2_b):
        import jax, jax.numpy as jnp
        import numpy as np
        from jax import lax
        EPS = 1e-05

        def haar_dwt(x):
            B, C, H, W = x.shape
            xr = x.reshape(B, C, H // 2, 2, W // 2, 2)
            x00 = xr[:, :, :, 0, :, 0]
            x01 = xr[:, :, :, 0, :, 1]
            x10 = xr[:, :, :, 1, :, 0]
            x11 = xr[:, :, :, 1, :, 1]
            ll = (x00 + x01 + x10 + x11) * 0.5
            lh = (x00 + x01 - x10 - x11) * 0.5
            hl = (x00 - x01 + x10 - x11) * 0.5
            hh = (x00 - x01 - x10 + x11) * 0.5
            return (ll, lh, hl, hh)

        def haar_idwt(ll, lh, hl, hh):
            y00 = (ll + lh + hl + hh) * 0.5
            y01 = (ll + lh - hl - hh) * 0.5
            y10 = (ll - lh + hl - hh) * 0.5
            y11 = (ll - lh - hl + hh) * 0.5
            B, C, H, W = ll.shape
            top = jnp.stack([y00, y01], axis=-1)
            bot = jnp.stack([y10, y11], axis=-1)
            y = jnp.stack([top, bot], axis=3)
            return y.reshape(B, C, 2 * H, 2 * W)

        def conv1x1(x, w, b):
            return jnp.einsum('bchw,oc->bohw', x, w) + b[None, :, None, None]

        def batchnorm(x, g, b):
            mu = jnp.mean(x, axis=(0, 2, 3), keepdims=True)
            var = jnp.var(x, axis=(0, 2, 3), keepdims=True)
            xh = (x - mu) * lax.rsqrt(var + EPS)
            return xh * g[None, :, None, None] + b[None, :, None, None]

        def layernorm_chw(x, g, b):
            mu = jnp.mean(x, axis=(1, 2, 3), keepdims=True)
            var = jnp.var(x, axis=(1, 2, 3), keepdims=True)
            xh = (x - mu) * lax.rsqrt(var + EPS)
            return xh * g[None, :, None, None] + b[None, :, None, None]

        def dwconv3x3(x, w, b):
            C = x.shape[1]
            y = lax.conv_general_dilated(x, w, (1, 1), [(1, 1), (1, 1)], dimension_numbers=('NCHW', 'OIHW', 'NCHW'), feature_group_count=C)
            return y + b[None, :, None, None]
        gelu = lambda x: jax.nn.gelu(x, approximate=False)
        ll, lh, hl, hh = haar_dwt(x)
        h = jnp.concatenate([ll, lh, hl, hh], axis=1)
        h = gelu(batchnorm(conv1x1(h, w_c1, b_c1), bn1_g, bn1_b))
        res = h
        o = dwconv3x3(h, dw_w, dw_b)
        o = layernorm_chw(o, gn_g, gn_b)
        o = conv1x1(o, pw1_w, pw1_b)
        o = gelu(o)
        o = conv1x1(o, pw2_w, pw2_b)
        h = o + res
        h = gelu(batchnorm(conv1x1(h, w_c2, b_c2), bn2_g, bn2_b))
        C = h.shape[1] // 4
        return haar_idwt(h[:, :C], h[:, C:2 * C], h[:, 2 * C:3 * C], h[:, 3 * C:])

    def _L1_conv_ref(input, kernel):
        import jax, jax.numpy as jnp
        from jax import lax
        import numpy as np
        B, C, H, W = (8, 128, 256, 256)
        PAD0, PAD1 = (2, 1)
        UPSAMPLE_FACTOR = 2

        def _make_kernel():
            k1 = jnp.array([1.0, 3.0, 3.0, 1.0], dtype=jnp.float32)
            k = k1[:, None] * k1[None, :]
            k = k / jnp.sum(k)
            k = k * UPSAMPLE_FACTOR ** 2
            return k
        c = input.shape[1]
        k = jnp.flip(kernel, (0, 1))
        w = jnp.broadcast_to(k[None, None], (c, 1) + k.shape)
        xp = jnp.pad(input, ((0, 0), (0, 0), (PAD0, PAD1), (PAD0, PAD1)))
        out = lax.conv_general_dilated(xp, w, window_strides=(1, 1), padding='VALID', dimension_numbers=('NCHW', 'OIHW', 'NCHW'), feature_group_count=c)
        return out

    def _gn(v, G=32, eps=1e-5):
        B_, C_, H_, W_ = v.shape
        g = v.reshape(B_, G, C_ // G, H_, W_)
        m = jnp.mean(g, axis=(2, 3, 4), keepdims=True)
        s = jnp.var(g, axis=(2, 3, 4), keepdims=True)
        return ((g - m) / jnp.sqrt(s + eps)).reshape(v.shape)

    def _ln_c(v, eps=1e-6):
        m = jnp.mean(v, axis=1, keepdims=True)
        s = jnp.var(v, axis=1, keepdims=True)
        return (v - m) / jnp.sqrt(s + eps)

    def _ln_t(v, eps=1e-5):
        m = jnp.mean(v, axis=-1, keepdims=True)
        s = jnp.var(v, axis=-1, keepdims=True)
        return (v - m) / jnp.sqrt(s + eps)

    def _to_tokens(v):
        B_, C_, H_, W_ = v.shape
        return v.reshape(B_, C_, H_ * W_).transpose(0, 2, 1)
    def _from_tokens(t, like):
        B_, C_, H_, W_ = like.shape
        return t.transpose(0, 2, 1).reshape(B_, C_, H_, W_)

    x = x + _L0_conv_ref(_gn(x), L0_conv_w_c1, L0_conv_b_c1, L0_conv_bn1_g, L0_conv_bn1_b, L0_conv_dw_w, L0_conv_dw_b, L0_conv_gn_g, L0_conv_gn_b, L0_conv_pw1_w, L0_conv_pw1_b, L0_conv_pw2_w, L0_conv_pw2_b, L0_conv_w_c2, L0_conv_b_c2, L0_conv_bn2_g, L0_conv_bn2_b)
    x = x + _L1_conv_ref(_gn(x), L1_conv_kernel)
    return x


_drawn_inputs = setup_inputs


def setup_inputs(seed=0):
    import zlib

    import numpy as np

    out = dict(_drawn_inputs(seed))
    spreads = {'L0_conv_b_c1': (0.0, 0.8),
     'L0_conv_bn1_g': (1.0, 0.2),
     'L0_conv_bn1_b': (0.0, 0.1),
     'L0_conv_dw_b': (0.0, 0.1),
     'L0_conv_gn_g': (1.0, 0.2),
     'L0_conv_gn_b': (0.0, 0.1),
     'L0_conv_pw1_b': (0.0, 0.292),
     'L0_conv_pw2_b': (0.0, 0.8),
     'L0_conv_b_c2': (0.0, 0.8),
     'L0_conv_bn2_g': (1.0, 0.2),
     'L0_conv_bn2_b': (0.0, 0.1)}
    factors = {}
    for name, (base, spread) in spreads.items():
        noise = np.random.default_rng([zlib.crc32(name.encode()), seed]).standard_normal(out[name].shape)
        drawn = base * np.exp(spread * noise) if base else spread * noise
        out[name] = jnp.asarray(drawn.astype(out[name].dtype))
    for name, factor in factors.items():
        out[name] = (out[name] * factor).astype(out[name].dtype)
    return out
```

```python
import numpy as np
import concourse.bass as bass
from concourse import mybir
from contextlib import ExitStack

F32 = mybir.dt.float32
F32R = mybir.dt.float32r
BF16 = mybir.dt.bfloat16
ALU = mybir.AluOpType
ACT = mybir.ActivationFunctionType
AX = mybir.AxisListType

B, C, H, W = 8, 128, 256, 256
HW = H * W
H2, W2 = H // 2, W // 2
HW2 = H2 * W2
GRP = 4
NG = C // GRP
EPS = 1e-5
BANK = 512
TAPS = 9
BN_W = 6

V_BC1, V_BN1G, V_BN1B, V_DWB, V_GNG, V_GNB, V_PW1B, V_PW2B = range(8)
V_BC2, V_BN2G, V_BN2B, V_DWW = 8, 12, 16, 20
V_ALL = V_DWW + TAPS

K_ID = 0
K_G4 = K_ID + C
K_GM = K_G4 + C
K_TM = K_GM + NG
K_HM = K_TM + 4 * 128
K_H1 = K_HM + 2 * 4 * 128
K_ALL = K_H1 + W

HALO_ROWS = 3
Q_STEP = 32
HALO_P = 2 * Q_STEP + 4 * HALO_ROWS


def shape_constants():
    k = np.zeros((128, K_ALL), np.float32)
    k[:, K_ID:K_ID + C] = np.eye(C)
    p = np.arange(128)
    k[:, K_G4:K_G4 + C] = (p[:, None] // GRP == p[None, :] // GRP) / GRP
    k[:, K_GM:K_GM + NG] = p[:, None] // GRP == np.arange(NG)[None, :]
    for kh in range(4):
        k[:, K_TM + kh * 128:K_TM + (kh + 1) * 128] = p[:, None] - p[None, :] == kh - 2
    for q in range(3):
        for kw in range(4):
            for r in range(HALO_ROWS):
                row = q * Q_STEP + kw * HALO_ROWS + r
                for t in range(2):
                    for m in ((127,), (0, 1))[t]:
                        kh = 126 + r - (128 * t + m) + 2
                        if 0 <= kh < 4 and (r == 2) == (t == 0):
                            k[row, K_HM + (t * 4 + kh) * 128 + m] = 1.0
                w = np.arange(W) + kw - 2
                k[row, K_H1:K_H1 + W] = (w >= 0) & (w < W)
    return k


class Chain:

    def __init__(self, engine, semaphore, base=0):
        self.engine, self.semaphore, self.base, self.n = engine, semaphore, base, 0

    def link(self, instruction):
        self.n += 1
        instruction.then_inc(self.semaphore, 1)
        self.engine.wait_ge(self.semaphore, self.base + self.n)


def build(nc, x, vec, wc1, pw1, pw2, wc2, kern, halo_k, const, out):
    z_d = nc.dram_tensor("z_scratch", (C, B, HW2), F32, kind="Internal").ap()
    u_d = nc.dram_tensor("u_scratch", (C, B, HW2), F32, kind="Internal").ap()
    y_d = nc.dram_tensor("y_scratch", (B, C, H, W), F32, kind="Internal").ap()
    with ExitStack() as keep:
        def sbk(name, shape, dt=F32):
            return keep.enter_context(nc.sbuf_tensor(name, shape, dt))

        K = sbk("constants", [128, K_ALL])
        V = sbk("vectors", [128, V_ALL])
        KR = sbk("blur_taps", [128, 16])
        HK = sbk("blur_halo_taps", [128, 4])
        neg_half = sbk("neg_half", [128, NG])
        n128 = sbk("mean_over_channels", [128, 128])
        quarter = sbk("quarter", [128, 128])
        x_gmean = sbk("x_group_mean", [128, B])
        x_cmean = sbk("x_channel_mean", [128, B])
        z_sum = sbk("z_sum", [128, B * 16])
        z_sq = sbk("z_sq", [128, B * 16])
        gram = sbk("gram", [128, C + 1])
        bn2_a = sbk("bn2_scale", [128, 4])
        bn2_d = sbk("bn2_shift", [128, 4])
        ll_sum = sbk("ll_sum", [128, B, 32])
        y_sq = sbk("y_sq", [128, B, 16])
        nm_b = sbk("neg_mean_all", [128, B, NG])
        rs_b = sbk("rstd_all", [128, B, NG])
        sem = lambda name: keep.enter_context(nc.semaphore(name))
        keepers = dict(sem=sem, K=K, V=V, KR=KR, HK=HK, neg_half=neg_half, n128=n128, quarter=quarter,
                       x_gmean=x_gmean, x_cmean=x_cmean, z_sum=z_sum, z_sq=z_sq, gram=gram,
                       bn2_a=bn2_a, bn2_d=bn2_d, ll_sum=ll_sum, y_sq=y_sq, nm_b=nm_b, rs_b=rs_b)
        phase_conv1(nc, keepers, x, vec, wc1, kern, halo_k, const, z_d)
        phase_mix(nc, keepers, pw1, pw2, z_d, u_d)
        phase_conv2(nc, keepers, wc2, x, u_d, y_d)
        phase_blur(nc, keepers, y_d, out)


ROWS1 = 16
CH1 = H // ROWS1
NS = 11
AGAIN = 6
LOADS = CH1 + AGAIN
LINKS1 = 5


def conv_position(load):
    return load - AGAIN


def phase_conv1(nc, kp, x, vec, wc1, kern, halo_k, const, z_d):
    K, V, n128 = kp["K"], kp["V"], kp["n128"]
    CW = ROWS1 * W
    ZW = CW // 4
    with ExitStack() as ctx:
        sb = lambda name, shape, dt=F32: ctx.enter_context(nc.sbuf_tensor(name, shape, dt))
        ps = lambda name, shape: ctx.enter_context(nc.psum_tensor(name, shape, F32))
        sem = kp["sem"]
        ring = sb("x_ring", [128, NS, CW])
        stats = sb("x_stats", [128, CH1 * CW // BANK, BN_W])
        w_ph = sb("w_phase", [128, 4, C])
        w_f = sb("w_folded", [128, 4, C])
        zt = sb("z_tile", [128, 2, ZW])
        w_sub = zt[:, 0, 0:4 * C].rearrange("p (s o) -> p s o", o=C)
        t_ab = zt[:, 1, 0:4 * C].rearrange("p (s o) -> p s o", o=C)
        mv = sb("x_mean_var", [128, 2])
        waiter = sb("waiter1", [128, 1])
        d = sb("x_dev", [128, 1])
        ve = sb("x_var_eps", [128, 1])
        rs = sb("x_rstd", [128, 1])
        negb = sb("group_mean_now", [128, 1])
        bias = sb("z_bias", [128, 1])
        zp = [ps(f"z_psum{i}", [128, ZW]) for i in range(3)]
        small = ps("small1", [128, 4])

        s_const = sem("const_loaded")
        s_set = sem("memsets_done")
        s_prep = sem("phase_weights_done")
        s_x = [sem(f"x_loaded{i}") for i in range(NS)]
        s_stat = sem("x_chunk_counted")
        s_conv = sem("x_chunk_convolved")
        s_link = sem("vector_link1")
        s_mv = sem("channel_stats_ready")
        s_avg = sem("group_average_ready")
        s_ve = sem("variance_ready")
        s_rs = sem("rstd_ready")
        s_fold = sem("weights_folded")
        s_bmm = sem("bias_product_ready")
        s_bias = sem("bias_ready")
        s_evac = sem("z_evacuated")
        s_sq = sem("z_squared")
        s_zst = [sem(f"z_stored{i}") for i in range(2)]

        xv = x.rearrange("b c h w -> b c (h w)")
        block = ctx.enter_context(nc.Block())

        def chunk_of(load):
            return load if load < CH1 else load - CH1

        @block.sync
        def _(sp):
            n = 0
            for dst, src in ((K[:], const), (V[:], vec), (w_sub, wc1), (kp["KR"][:], kern),
                             (kp["HK"][:], halo_k)):
                sp.dma_start(dst, src).then_inc(s_const, 16)
            with sp.Fori(0, B) as b:
                for load in range(LOADS):
                    before = load - NS
                    if 0 <= before < AGAIN:
                        sp.wait_ge(s_stat, b * CH1 + before + 1)
                    elif before >= 0:
                        sp.wait_ge(s_conv, b * CH1 + CH1 + conv_position(before) + 1)
                    else:
                        sp.wait_ge(s_conv, b * CH1 + conv_position(load + NS) + 1)
                    c0 = chunk_of(load) * CW
                    sp.dma_start(ring[:, load % NS, :],
                                 xv[bass.ds(b, 1), :, c0:c0 + CW].rearrange("b c n -> c (b n)")
                                 ).then_inc(s_x[load % NS], 16)

        @block.gpsimd
        def _(pool):
            pool.memset(kp["neg_half"][:], -0.5).then_inc(s_set, 1)
            pool.memset(n128[:], 1.0 / C).then_inc(s_set, 1)
            pool.memset(kp["quarter"][:], 1.0 / GRP).then_inc(s_set, 1)
            pool.wait_ge(s_set, 3)
            with pool.Fori(0, B) as b:
                pool.wait_ge(s_ve, b + 1)
                nc.gpsimd.tensor_tensor(rs[:], ve[:], kp["neg_half"][:, 0:1], ALU.pow).then_inc(s_rs, 1)

        @block.vector
        def _(dve):
            dve.wait_ge(s_const, 16 * 5)
            pair = w_sub.rearrange("p (a b) o -> p a b o", b=2)
            nc.vector.tensor_tensor(t_ab[:, 0:2, :], pair[:, :, 0, :], pair[:, :, 1, :], ALU.add).then_inc(s_prep, 1)
            nc.vector.tensor_tensor(t_ab[:, 2:4, :], pair[:, :, 0, :], pair[:, :, 1, :], ALU.subtract).then_inc(s_prep, 1)
            dve.wait_ge(s_prep, 2)
            tp = t_ab.rearrange("p (a b) o -> p a b o", b=2)
            wp = w_ph[:].rearrange("p (a b) o -> p a b o", b=2)
            nc.vector.tensor_tensor(wp[:, :, 0, :], tp[:, :, 0, :], tp[:, :, 1, :], ALU.add).then_inc(s_prep, 1)
            nc.vector.tensor_tensor(wp[:, :, 1, :], tp[:, :, 0, :], tp[:, :, 1, :], ALU.subtract).then_inc(s_prep, 1)
            dve.wait_ge(s_prep, 4)
            nc.vector.tensor_scalar(w_ph[:], w_ph[:], 0.5, None, ALU.mult).then_inc(s_prep, 1)
            dve.wait_ge(s_prep, 5)
            with dve.Fori(0, B) as b:
                for c in range(CH1):
                    dve.wait_ge(s_x[c % NS], b * 32 + 16 * (c // NS + 1))
                    for k in range(CW // BANK):
                        ins = nc.vector.bn_stats(stats[:, c * (CW // BANK) + k, :],
                                                 ring[:, c % NS, k * BANK:(k + 1) * BANK])
                    ins.then_inc(s_stat, 1)
                dve.wait_ge(s_stat, b * CH1 + CH1)
                nc.vector.memset(waiter[:], 0.0)
                nc.vector.bn_aggr(mv[:], stats[:].rearrange("p a b -> p (a b)")).then_inc(s_mv, 1)
                dve.wait_ge(s_mv, b * 2 + 1)
                ch = Chain(dve, s_link, b * LINKS1)
                dve.wait_ge(s_avg, b * 2 + 1)
                ch.link(nc.vector.tensor_copy(kp["x_gmean"][:, bass.ds(b, 1)], small[:, 0:1]))
                ch.link(nc.vector.tensor_copy(kp["x_cmean"][:, bass.ds(b, 1)], mv[:, 0:1]))
                ch.link(nc.vector.tensor_tensor(d[:], mv[:, 0:1], small[:, 0:1], ALU.subtract))
                ch.link(nc.vector.scalar_tensor_tensor(d[:], d[:], d[:], mv[:, 1:2], ALU.mult, ALU.add))
                ch.link(nc.vector.tensor_copy(negb[:], small[:, 0:1]))
                nc.vector.tensor_copy(mv[:, 1:2], d[:]).then_inc(s_mv, 1)
                dve.wait_ge(s_avg, b * 2 + 2)
                nc.vector.tensor_scalar(ve[:], small[:, 1:2], EPS, None, ALU.add).then_inc(s_ve, 1)
                dve.wait_ge(s_rs, b + 1)
                nc.vector.tensor_scalar(w_f[:], w_ph[:], rs[:], None, ALU.mult).then_inc(s_fold, 1)
                dve.wait_ge(s_bmm, b + 1)
                dve.wait_ge(s_sq, b * CH1 + 3)
                nc.vector.tensor_scalar(bias[:], small[:, 2:3], -1.0, None, ALU.mult).then_inc(s_bias, 1)
                assert ch.n == LINKS1

        @block.tensor
        def _(pe):
            pe.sem_inc(s_conv, CH1)
            pe.wait_ge(s_const, 16 * 5)
            pe.wait_ge(s_set, 3)
            with pe.Fori(0, B) as b:
                pe.wait_ge(s_mv, b * 2 + 1)
                nc.tensor.matmul(small[:, 0:1], K[:, K_G4:K_G4 + C], mv[:, 0:1], start=True, stop=True).then_inc(s_avg, 1)
                pe.wait_ge(s_mv, b * 2 + 2)
                nc.tensor.matmul(small[:, 1:2], K[:, K_G4:K_G4 + C], mv[:, 1:2], start=True, stop=True).then_inc(s_avg, 1)
                pe.wait_ge(s_fold, b + 1)
                for p in range(4):
                    ins = nc.tensor.matmul(small[:, 2:3], w_f[:, p, :], negb[:], start=(p == 0), stop=(p == 3))
                ins.then_inc(s_bmm, 1)
                for q in range(CH1):
                    load = q + AGAIN
                    pe.wait_ge(s_x[load % NS], b * 32 + 16 * (load // NS + 1))
                    pe.wait_ge(s_sq, b * CH1 + max(q, 2) + 1)
                    px = ring[:, load % NS, :].rearrange("c (i a j e) -> c a e i j", a=2, e=2, j=W2)
                    for half in range(2):
                        rows = slice(half * 4, half * 4 + 4)
                        for p in range(4):
                            ins = nc.tensor.matmul(zp[q % 3][:, half * BANK:(half + 1) * BANK],
                                                   w_f[:, p, :], px[:, p // 2, p % 2, rows, :],
                                                   start=(p == 0), stop=(p == 3))
                    ins.then_inc(s_conv, 1)

        @block.scalar
        def _(act):
            zv = z_d.rearrange("c b n -> b c n")
            act.sem_inc(s_sq, 3)
            for i in range(2):
                act.sem_inc(s_zst[i], 16)
            with act.Fori(0, B) as b:
                act.wait_ge(s_bias, b + 1)
                for q in range(CH1):
                    act.wait_ge(s_conv, b * CH1 + CH1 + q + 1)
                    act.wait_ge(s_zst[q % 2], b * 16 * (CH1 // 2) + 16 * (q // 2 + 1))
                    nc.scalar.activation(zt[:, q % 2, :], zp[q % 3][:], ACT.Identity, bias=bias[:],
                                         accum_out=kp["z_sum"][:, bass.ds(b * CH1 + q, 1)]).then_inc(s_evac, 1)
                    act.wait_ge(s_evac, b * CH1 + q + 1)
                    nc.scalar.activation(zp[q % 3][:], zp[q % 3][:], ACT.Square, bias=bias[:],
                                         accum_out=kp["z_sq"][:, bass.ds(b * CH1 + q, 1)]).then_inc(s_sq, 1)
                    chunk = chunk_of(q + AGAIN)
                    act.dma_start(zv[bass.ds(b, 1), :, chunk * ZW:(chunk + 1) * ZW].rearrange("b c n -> c (b n)"),
                                  zt[:, q % 2, :]).then_inc(s_zst[q % 2], 16)
            for i in range(2):
                act.wait_ge(s_zst[i], 16 + 16 * B * CH1 // 2)


R2 = BANK // W2
STEPS = H2 // R2
PE_TAPS = 5
LINKS_LN = 6


def phase_mix(nc, kp, pw1, pw2, z_d, u_d):
    K, V, n128, neg_half = kp["K"], kp["V"], kp["n128"], kp["neg_half"]
    gram = kp["gram"]
    DVE_TAPS = TAPS - PE_TAPS
    with ExitStack() as ctx:
        sb = lambda name, shape, dt=F32: ctx.enter_context(nc.sbuf_tensor(name, shape, dt))
        ps = lambda name, shape: ctx.enter_context(nc.psum_tensor(name, shape, F32))
        sem = kp["sem"]
        plane = sb("h_plane", [128, H2 + 2, W2 + 2])
        o_buf = sb("depthwise_out", [128, STEPS, BANK])
        z_in = sb("z_in", [128, 4, BANK])
        diag = sb("tap_diagonals", [128, PE_TAPS, C])
        w1 = sb("pw1_weights", [128, C])
        w1f = sb("pw1_folded", [128, C])
        w2 = sb("pw2_weights", [128, C])
        v_t = sb("gelu1_out", [128, 2, BANK])
        u_t = sb("u_tile", [128, 4, BANK])
        u_tr = sb("u_transposed", [128, 2, 4, C + 1])
        bst = sb("o_stats", [128, STEPS, BN_W])
        mv = sb("o_mean_var", [128, 2])
        waiter = sb("waiter2", [128, 1])
        t = sb("small_columns", [128, 8])
        bn1_a = sb("bn1_scale", [128, 1])
        bn1_d = sb("bn1_shift", [128, 1])
        b1 = sb("pw1_bias", [128, 1])
        dw_p = [ps(f"dw_psum{i}", [128, BANK]) for i in range(2)]
        p1_p = [ps(f"pw1_psum{i}", [128, BANK]) for i in range(2)]
        p2_p = ps("pw2_psum", [128, BANK])
        tr_p = [ps(f"transpose_psum{i}", [128, BANK]) for i in range(2)]
        g_p = ps("gram_psum", [128, BANK])
        small = g_p[:, 256:260]

        s_w = sem("pw_weights_loaded")
        s_zero = sem("plane_zeroed")
        s_lk = sem("vector_link2")
        s_lk_tap = sem("tap_link")
        s_lk_ln = sem("layer_norm_link")
        s_pow = sem("pow_wanted2")
        s_rs = sem("rstd_ready2")
        s_bn1 = sem("bn1_ready")
        s_z = [sem(f"z_loaded{i}") for i in range(4)]
        s_h = sem("h_rows_ready")
        s_dw = sem("dw_psum_ready")
        s_o = sem("o_stats_done")
        s_lnm = sem("ln_means_wanted")
        s_lna = sem("ln_average_ready")
        s_ln = sem("pw1_folded_ready")
        s_lnb = sem("pw1_bias_product")
        s_b1 = sem("pw1_bias_ready")
        s_p1 = sem("pw1_ready")
        s_g1 = sem("gelu1_ready")
        s_p2 = sem("pw2_ready")
        s_u = sem("u_ready")
        s_tr = sem("u_transposed_psum")
        s_ut = sem("u_transposed_sbuf")
        s_gm = sem("gram_step_done")
        s_ust = [sem(f"u_stored{i}") for i in range(4)]

        zv = z_d.rearrange("c b n -> b c n")
        uv = u_d.rearrange("c b n -> b c n")
        block = ctx.enter_context(nc.Block())

        def tap(k, j):
            kh, kw = k // 3, k % 3
            return plane[:, j * R2 + kh:j * R2 + kh + R2, kw:kw + W2]

        def rows_of(j):
            return plane[:, 1 + j * R2:1 + (j + 1) * R2, 1:1 + W2]

        @block.sync
        def _(sp):
            sp.dma_start(w1[:], pw1).then_inc(s_w, 16)
            sp.dma_start(w2[:], pw2).then_inc(s_w, 16)
            with sp.Fori(0, B) as b:
                for j in range(STEPS):
                    sp.wait_ge(s_h, b * (STEPS + 1) + j + 1)
                    sp.dma_start(z_in[:, j % 4, :],
                                 zv[bass.ds(b, 1), :, j * BANK:(j + 1) * BANK].rearrange("b c n -> c (b n)")
                                 ).then_inc(s_z[j % 4], 16)
                for j in range(STEPS):
                    sp.wait_ge(s_u, b * STEPS + j + 1)
                    sp.dma_start(uv[bass.ds(b, 1), :, j * BANK:(j + 1) * BANK].rearrange("b c n -> c (b n)"),
                                 u_t[:, j % 4, :]).then_inc(s_ust[j % 4], 16)
            for i in range(4):
                sp.wait_ge(s_ust[i], 16 + 16 * B * STEPS // 4)

        @block.gpsimd
        def _(pool):
            pool.memset(plane[:].rearrange("p a b -> p (a b)"), 0.0).then_inc(s_zero, 1)
            pool.memset(u_tr[:, :, :, C:C + 1], 1.0).then_inc(s_zero, 1)
            pool.wait_ge(s_pow, 1)
            nc.gpsimd.tensor_tensor(t[:, 3:4], t[:, 2:3], neg_half[:, 0:1], ALU.pow).then_inc(s_rs, 1)
            with pool.Fori(0, B) as b:
                pool.wait_ge(s_pow, b + 2)
                nc.gpsimd.tensor_tensor(t[:, 3:4], t[:, 2:3], neg_half[:, 0:1], ALU.pow).then_inc(s_rs, 1)

        @block.vector
        def _(dve):
            N = float(B * HW2)
            lk = Chain(dve, s_lk)
            lk.link(nc.vector.memset(gram[:], 0.0))
            lk.link(nc.vector.reduce_sum(t[:, 0:1], kp["z_sum"][:], AX.X))
            lk.link(nc.vector.reduce_sum(t[:, 1:2], kp["z_sq"][:], AX.X))
            lk.link(nc.vector.tensor_scalar(t[:, 0:2], t[:, 0:2], 1.0 / N, None, ALU.mult))
            lk.link(nc.vector.tensor_tensor(t[:, 4:5], t[:, 0:1], t[:, 0:1], ALU.mult))
            lk.link(nc.vector.tensor_tensor(t[:, 4:5], t[:, 1:2], t[:, 4:5], ALU.subtract))
            nc.vector.tensor_scalar(t[:, 2:3], t[:, 4:5], EPS, None, ALU.add).then_inc(s_pow, 1)
            lk.link(nc.vector.tensor_tensor(t[:, 5:6], t[:, 0:1], V[:, V_BC1:V_BC1 + 1], ALU.add))
            lk.link(nc.vector.tensor_tensor(t[:, 6:7], V[:, V_BC1:V_BC1 + 1], t[:, 5:6], ALU.subtract))
            dve.wait_ge(s_rs, 1)
            lk.link(nc.vector.tensor_tensor(bn1_a[:], t[:, 3:4], V[:, V_BN1G:V_BN1G + 1], ALU.mult))
            nc.vector.scalar_tensor_tensor(bn1_d[:], t[:, 6:7], bn1_a[:], V[:, V_BN1B:V_BN1B + 1],
                                           ALU.mult, ALU.add).then_inc(s_bn1, 1)
            for k in range(PE_TAPS):
                nc.vector.tensor_scalar(diag[:, k, :], K[:, K_ID:K_ID + C], V[:, V_DWW + k:V_DWW + k + 1],
                                        None, ALU.mult).then_inc(s_bn1, 1)
            dve.wait_ge(s_w, 32)
            for i in range(4):
                dve.sem_inc(s_ust[i], 16)
            with dve.Fori(0, B) as b:
                taps = Chain(dve, s_lk_tap, b * STEPS * DVE_TAPS)
                for j in range(STEPS):
                    dve.wait_ge(s_dw, b * STEPS + j + 1)
                    for n, k in enumerate(range(PE_TAPS, TAPS)):
                        ins = nc.vector.scalar_tensor_tensor(
                            o_buf[:, j, :].rearrange("p (r c) -> p r c", c=W2), tap(k, j),
                            V[:, V_DWW + k:V_DWW + k + 1],
                            (dw_p[j % 2][:] if n == 0 else o_buf[:, j, :]).rearrange("p (r c) -> p r c", c=W2),
                            ALU.mult, ALU.add)
                        taps.link(ins)
                    nc.vector.bn_stats(bst[:, j, :], o_buf[:, j, :]).then_inc(s_o, 1)
                ln = Chain(dve, s_lk_ln, b * LINKS_LN)
                dve.wait_ge(s_o, (b + 1) * STEPS)
                nc.vector.memset(waiter[:], 0.0)
                ln.link(nc.vector.bn_aggr(mv[:], bst[:].rearrange("p a b -> p (a b)")))
                nc.vector.tensor_tensor(t[:, 0:1], mv[:, 0:1], V[:, V_DWB:V_DWB + 1], ALU.add).then_inc(s_lnm, 1)
                dve.wait_ge(s_lna, b * 2 + 1)
                dve.wait_ge(s_lnm, b * 2 + 1)
                ln.link(nc.vector.tensor_tensor(t[:, 4:5], t[:, 0:1], small[:, 0:1], ALU.subtract))
                ln.link(nc.vector.tensor_tensor(t[:, 5:6], V[:, V_DWB:V_DWB + 1], small[:, 0:1], ALU.subtract))
                nc.vector.scalar_tensor_tensor(t[:, 1:2], t[:, 4:5], t[:, 4:5], mv[:, 1:2],
                                               ALU.mult, ALU.add).then_inc(s_lnm, 1)
                dve.wait_ge(s_lna, b * 2 + 2)
                nc.vector.tensor_scalar(t[:, 2:3], small[:, 1:2], EPS, None, ALU.add).then_inc(s_pow, 1)
                dve.wait_ge(s_rs, b + 2)
                ln.link(nc.vector.tensor_tensor(t[:, 6:7], t[:, 3:4], V[:, V_GNG:V_GNG + 1], ALU.mult))
                ln.link(nc.vector.tensor_scalar(w1f[:], w1[:], t[:, 6:7], None, ALU.mult))
                nc.vector.scalar_tensor_tensor(t[:, 7:8], t[:, 5:6], t[:, 6:7], V[:, V_GNB:V_GNB + 1],
                                               ALU.mult, ALU.add).then_inc(s_ln, 1)
                dve.wait_ge(s_lnb, b + 1)
                nc.vector.tensor_tensor(b1[:], small[:, 2:3], V[:, V_PW1B:V_PW1B + 1], ALU.add).then_inc(s_b1, 1)
                for j in range(STEPS):
                    dve.wait_ge(s_p2, b * STEPS + j + 1)
                    dve.wait_ge(s_ust[j % 4], b * 16 * (STEPS // 4) + 16 * (j // 4 + 1))
                    if j >= 4:
                        dve.wait_ge(s_tr, b * STEPS + j - 3)
                    nc.vector.scalar_tensor_tensor(
                        u_t[:, j % 4, :].rearrange("p (r c) -> p r c", c=W2),
                        p2_p[:].rearrange("p (r c) -> p r c", c=W2), V[:, V_PW2B:V_PW2B + 1],
                        rows_of(j), ALU.add, ALU.add).then_inc(s_u, 1)
                dve.wait_ge(s_gm, (b + 1) * STEPS)
                ln.link(nc.vector.tensor_tensor(gram[:], gram[:], g_p[:, 0:C + 1], ALU.add))
                assert ln.n == LINKS_LN

        @block.tensor
        def _(pe):
            pe.wait_ge(s_bn1, 1 + PE_TAPS)
            pe.wait_ge(s_w, 32)
            pe.wait_ge(s_zero, 2)
            with pe.Fori(0, B) as b:
                for j in range(STEPS):
                    pe.wait_ge(s_h, 4 + b * (STEPS + 1) + j + 2)
                    if j >= 2:
                        pe.wait_ge(s_lk_tap, b * STEPS * DVE_TAPS + (j - 2) * DVE_TAPS + 1)
                    for k in range(PE_TAPS):
                        ins = nc.tensor.matmul(dw_p[j % 2][:], diag[:, k, :], tap(k, j),
                                               start=(k == 0), stop=(k == PE_TAPS - 1))
                    ins.then_inc(s_dw, 1)
                pe.wait_ge(s_lnm, b * 2 + 1)
                nc.tensor.matmul(small[:, 0:1], n128[:], t[:, 0:1], start=True, stop=True).then_inc(s_lna, 1)
                pe.wait_ge(s_lnm, b * 2 + 2)
                nc.tensor.matmul(small[:, 1:2], n128[:], t[:, 1:2], start=True, stop=True).then_inc(s_lna, 1)
                pe.wait_ge(s_ln, b + 1)
                nc.tensor.matmul(small[:, 2:3], w1[:], t[:, 7:8], start=True, stop=True).then_inc(s_lnb, 1)

                def pw1_step(j):
                    if j >= 2:
                        pe.wait_ge(s_g1, b * STEPS + j - 1)
                    nc.tensor.matmul(p1_p[j % 2][:], w1f[:], o_buf[:, j, :], start=True, stop=True).then_inc(s_p1, 1)

                def pw2_step(j):
                    pe.wait_ge(s_g1, b * STEPS + j + 1)
                    if j >= 1:
                        pe.wait_ge(s_u, b * STEPS + j)
                    nc.tensor.matmul(p2_p[:], w2[:], v_t[:, j % 2, :], start=True, stop=True).then_inc(s_p2, 1)

                def transpose_step(j):
                    pe.wait_ge(s_u, b * STEPS + j + 1)
                    if j >= 2:
                        pe.wait_ge(s_ut, b * STEPS + j - 1)
                    for q in range(4):
                        ins = nc.tensor.transpose(tr_p[j % 2][:, q * C:(q + 1) * C],
                                                  u_t[:, j % 4, q * C:(q + 1) * C], K[:, K_ID:K_ID + C])
                    ins.then_inc(s_tr, 1)

                def gram_step(j):
                    pe.wait_ge(s_ut, b * STEPS + j + 1)
                    for q in range(4):
                        ins = nc.tensor.matmul(g_p[:, 0:C + 1], u_tr[:, j % 2, q, 0:C], u_tr[:, j % 2, q, :],
                                               start=(j == 0 and q == 0), stop=(j == STEPS - 1 and q == 3))
                    ins.then_inc(s_gm, 1)

                pw1_step(0)
                for j in range(STEPS + 2):
                    if j + 1 < STEPS:
                        pw1_step(j + 1)
                    if j < STEPS:
                        pw2_step(j)
                    if 1 <= j <= STEPS:
                        transpose_step(j - 1)
                    if j >= 2:
                        gram_step(j - 2)

        @block.scalar
        def _(act):
            act.sem_inc(s_h, 4)
            act.wait_ge(s_bn1, 1)
            act.wait_ge(s_zero, 2)
            with act.Fori(0, B) as b:
                for j in range(STEPS):
                    act.wait_ge(s_z[j % 4], b * 16 * (STEPS // 4) + 16 * (j // 4 + 1))
                    nc.scalar.activation(rows_of(j), z_in[:, j % 4, :].rearrange("p (r c) -> p r c", c=W2),
                                         ACT.Gelu, scale=bn1_a[:], bias=bn1_d[:]).then_inc(s_h, 1)
                act.wait_ge(s_h, 4 + b * (STEPS + 1) + STEPS)
                act.sem_inc(s_h, 1)
                act.wait_ge(s_b1, b + 1)

                def evacuate(j):
                    act.wait_ge(s_tr, b * STEPS + j + 1)
                    if j >= 2:
                        act.wait_ge(s_gm, b * STEPS + j - 1)
                    nc.scalar.activation(u_tr[:, j % 2, :, 0:C], tr_p[j % 2][:].rearrange("p (q c) -> p q c", c=C),
                                         ACT.Copy).then_inc(s_ut, 1)

                for j in range(STEPS):
                    act.wait_ge(s_p1, b * STEPS + j + 1)
                    if j >= 2:
                        act.wait_ge(s_p2, b * STEPS + j - 1)
                    nc.scalar.activation(v_t[:, j % 2, :], p1_p[j % 2][:], ACT.Gelu, bias=b1[:]).then_inc(s_g1, 1)
                    if j >= 1:
                        evacuate(j - 1)
                evacuate(STEPS - 1)


ROWS3 = 16
UNITS3 = H // ROWS3
UW = ROWS3 * W // 4


def phase_conv2(nc, kp, wc2, x, u_d, y_d):
    K, V, neg_half, gram = kp["K"], kp["V"], kp["neg_half"], kp["gram"]
    bn2_a, bn2_d = kp["bn2_a"], kp["bn2_d"]
    with ExitStack() as ctx:
        sb = lambda name, shape, dt=F32: ctx.enter_context(nc.sbuf_tensor(name, shape, dt))
        ps = lambda name, shape: ctx.enter_context(nc.psum_tensor(name, shape, F32))
        sem = kp["sem"]
        w = sb("w_conv2", [128, 4 * C])
        prod = sb("w_products", [128, 4 * C])
        cov = sb("u_covariance", [128, C])
        mean_u = sb("u_mean", [128, 1])
        mean_row = sb("u_mean_row", [1, C])
        ones = sb("ones_column", [128, 1])
        t4 = sb("four_columns", [128, 6, 4])
        neg_gm = sb("neg_group_mean", [128, B])
        x_t = sb("x_tile", [128, 4, ROWS3 * W])
        u_t = sb("u_in", [128, 4, UW])
        g_t = sb("gelu2_out", [128, 2, 4, UW])
        s_t = sb("pair_sums", [128, 2, 4, UW])
        junk = sb("junk3", [128, ROWS3 * W], BF16)
        cp = [ps(f"conv2_psum{i}", [128, 4, BANK]) for i in range(2)]

        s_w = sem("conv2_weights_loaded")
        s_lk = sem("vector_link3")
        s_v = sem("vector_result3")
        s_p = sem("tensor_result3")
        s_rs = sem("rstd_ready3")
        s_bn2 = sem("bn2_ready")
        s_x = [sem(f"x_in{i}") for i in range(4)]
        s_u = [sem(f"u_in_loaded{i}") for i in range(4)]
        s_mm = sem("conv2_half_done")
        s_ge = sem("gelu2_half_done")
        s_bf = sem("pair_sums_done")
        s_half = sem("residual_added")
        s_y = sem("y_ready")
        s_sq = sem("y_squared")
        s_yst = [sem(f"y_stored{i}") for i in range(4)]

        uv = u_d.rearrange("c b n -> b c n")
        xv = x.rearrange("b c h w -> b c (h w)")
        yv = y_d.rearrange("b c h w -> b c (h w)")
        XW = ROWS3 * W
        block = ctx.enter_context(nc.Block())

        @block.sync
        def _(sp):
            sp.dma_start(w[:], wc2).then_inc(s_w, 16)
            for i in range(4):
                sp.sem_inc(s_yst[i], 16)
            with sp.Fori(0, B) as b:
                for k in range(UNITS3):
                    i = k % 4
                    sp.wait_ge(s_mm, b * 2 * UNITS3 + 2 * k + 2)
                    sp.dma_start(u_t[:, i, :], uv[bass.ds(b, 1), :, k * UW:(k + 1) * UW].rearrange("b c n -> c (b n)")
                                 ).then_inc(s_u[i], 16)
                    sp.wait_ge(s_yst[i], b * 16 * (UNITS3 // 4) + 16 * (k // 4 + 1))
                    sp.dma_start(x_t[:, i, :], xv[bass.ds(b, 1), :, k * XW:(k + 1) * XW].rearrange("b c n -> c (b n)")
                                 ).then_inc(s_x[i], 16)

        @block.gpsimd
        def _(pool):
            pool.wait_ge(s_v, 5)
            nc.gpsimd.tensor_tensor(t4[:, 2, :], t4[:, 1, :], neg_half[:, 0:4], ALU.pow).then_inc(s_rs, 1)
            pool.sem_inc(s_bf, 2)
            with pool.Fori(0, B) as b:
                for k in range(UNITS3):
                    pool.wait_ge(s_ge, b * 2 * UNITS3 + 2 * k + 4)
                    pool.wait_ge(s_y, b * UNITS3 + k + 1)
                    gp = g_t[:, k % 2].rearrange("p (a b) n -> p a b n", b=2)
                    nc.gpsimd.tensor_tensor(s_t[:, k % 2, 0:2, :], gp[:, :, 0, :], gp[:, :, 1, :], ALU.add)
                    nc.gpsimd.tensor_tensor(s_t[:, k % 2, 2:4, :], gp[:, :, 0, :], gp[:, :, 1, :],
                                            ALU.subtract).then_inc(s_bf, 1)

        @block.vector
        def _(dve):
            N = float(B * HW2)
            lk = Chain(dve, s_lk)
            dve.sem_inc(s_y, 2)
            lk.link(nc.vector.memset(ones[:], 1.0))
            lk.link(nc.vector.tensor_scalar(neg_gm[:], kp["x_gmean"][:], -1.0, None, ALU.mult))
            nc.vector.tensor_scalar(mean_u[:], gram[:, C:C + 1], 1.0 / N, None, ALU.mult).then_inc(s_v, 1)
            dve.wait_ge(s_p, 1)
            nc.vector.tensor_copy(mean_row[:], cp[0][0:1, 0, 0:C]).then_inc(s_v, 1)
            dve.wait_ge(s_p, 2)
            nc.vector.scalar_tensor_tensor(cov[:], gram[:, 0:C], 1.0 / N, cp[0][:, 1, 0:C],
                                           ALU.mult, ALU.subtract).then_inc(s_v, 1)
            dve.wait_ge(s_p, 3)
            nc.vector.tensor_tensor(prod[:], w[:], cp[0][:, 2, :], ALU.mult).then_inc(s_v, 1)
            dve.wait_ge(s_p, 4)
            b2 = V[:, V_BC2:V_BC2 + 4]
            lk.link(nc.vector.tensor_tensor(t4[:, 0, :], cp[0][:, 3, 0:4], b2, ALU.add))
            nc.vector.tensor_scalar(t4[:, 1, :], cp[0][:, 3, 4:8], EPS, None, ALU.add).then_inc(s_v, 1)
            lk.link(nc.vector.tensor_tensor(t4[:, 3, :], b2, t4[:, 0, :], ALU.subtract))
            dve.wait_ge(s_rs, 1)
            lk.link(nc.vector.tensor_tensor(bn2_a[:], t4[:, 2, :], V[:, V_BN2G:V_BN2G + 4], ALU.mult))
            lk.link(nc.vector.tensor_tensor(t4[:, 4, :], t4[:, 3, :], bn2_a[:], ALU.mult))
            nc.vector.tensor_tensor(bn2_d[:], t4[:, 4, :], V[:, V_BN2B:V_BN2B + 4], ALU.add).then_inc(s_bn2, 1)
            with dve.Fori(0, B) as b:
                for k in range(UNITS3):
                    i = k % 4
                    dve.wait_ge(s_bf, b * UNITS3 + k + 3)
                    dve.wait_ge(s_x[i], b * 16 * (UNITS3 // 4) + 16 * (k // 4 + 1))
                    xp = x_t[:, i, :].rearrange("c (i a j e) -> c a e i j", a=2, e=2, j=W2)
                    sums = s_t[:, k % 2].rearrange("c s (i j) -> c s i j", j=W2)
                    for a in range(2):
                        for e in range(2):
                            ins = nc.vector.scalar_tensor_tensor(xp[:, a, e], sums[:, 2 * a], 0.5, xp[:, a, e],
                                                                 ALU.mult, ALU.add)
                    ins.then_inc(s_half, 1)
                    dve.wait_ge(s_half, b * UNITS3 + k + 1)
                    for a in range(2):
                        for e in range(2):
                            ins = nc.vector.scalar_tensor_tensor(xp[:, a, e], sums[:, 2 * a + 1], (0.5, -0.5)[e],
                                                                 xp[:, a, e], ALU.mult, ALU.add)
                    ins.then_inc(s_y, 1)

        @block.tensor
        def _(pe):
            pe.sem_inc(s_mm, 8)
            pe.wait_ge(s_w, 16)
            pe.wait_ge(s_v, 1)
            nc.tensor.matmul(cp[0][0:1, 0, 0:C], mean_u[:], K[:, K_ID:K_ID + C], start=True, stop=True).then_inc(s_p, 1)
            pe.wait_ge(s_v, 2)
            nc.tensor.matmul(cp[0][:, 1, 0:C], mean_row[:], mean_row[:], start=True, stop=True).then_inc(s_p, 1)
            pe.wait_ge(s_v, 3)
            nc.tensor.matmul(cp[0][:, 2, :], cov[:], w[:], start=True, stop=True).then_inc(s_p, 1)
            pe.wait_ge(s_v, 4)
            for s in range(4):
                nc.tensor.matmul(cp[0][:, 3, s:s + 1], w[:, s * C:(s + 1) * C], mean_u[:], start=True, stop=True)
                ins = nc.tensor.matmul(cp[0][:, 3, 4 + s:5 + s], prod[:, s * C:(s + 1) * C], ones[:], start=True, stop=True)
            ins.then_inc(s_p, 1)
            pe.wait_ge(s_bn2, 1)
            with pe.Fori(0, B) as b:
                for k in range(UNITS3):
                    i = k % 4
                    pe.wait_ge(s_u[i], b * 16 * (UNITS3 // 4) + 16 * (k // 4 + 1))
                    for h in range(2):
                        pe.wait_ge(s_ge, b * 2 * UNITS3 + 2 * k + h + 1)
                        for s in range(4):
                            ins = nc.tensor.matmul(cp[h][:, s, :], w[:, s * C:(s + 1) * C],
                                                   u_t[:, i, h * BANK:(h + 1) * BANK], start=True, stop=True)
                        ins.then_inc(s_mm, 1)

        @block.scalar
        def _(act):
            act.sem_inc(s_ge, 2)
            act.wait_ge(s_bn2, 1)
            with act.Fori(0, B) as b:
                def finish(k):
                    i = k % 4
                    act.wait_ge(s_y, b * UNITS3 + k + 3)
                    nc.scalar.activation(junk[:], x_t[:, i, :], ACT.Square, bias=neg_gm[:, bass.ds(b, 1)],
                                         accum_out=kp["y_sq"][:, bass.ds(b, 1), k]).then_inc(s_sq, 1)
                    act.wait_ge(s_sq, b * UNITS3 + k + 1)
                    act.dma_start(yv[bass.ds(b, 1), :, k * XW:(k + 1) * XW].rearrange("b c n -> c (b n)"),
                                  x_t[:, i, :]).then_inc(s_yst[i], 16)

                for k in range(UNITS3):
                    act.wait_ge(s_bf, b * UNITS3 + k + 1)
                    for h in range(2):
                        act.wait_ge(s_mm, b * 2 * UNITS3 + 2 * k + h + 9)
                        for s in range(4):
                            more = {"accum_out": kp["ll_sum"][:, bass.ds(b, 1), 2 * k + h]} if s == 0 else {}
                            ins = nc.scalar.activation(g_t[:, k % 2, s, h * BANK:(h + 1) * BANK], cp[h][:, s, :],
                                                       ACT.Gelu, scale=bn2_a[:, s:s + 1], bias=bn2_d[:, s:s + 1], **more)
                        ins.then_inc(s_ge, 1)
                    if k >= 1:
                        finish(k - 1)
                finish(UNITS3 - 1)
            for i in range(4):
                act.wait_ge(s_yst[i], 16 + 16 * B * UNITS3 // 4)


PADW = W + 4
BODY4 = 8
UNITS4 = B * NG
HCH = 16


def phase_blur(nc, kp, y_d, out):
    K, neg_half = kp["K"], kp["neg_half"]
    nm_b, rs_b = kp["nm_b"], kp["rs_b"]
    LAST = UNITS4 // BODY4 - 1
    with ExitStack() as ctx:
        sb = lambda name, shape, dt=F32: ctx.enter_context(nc.sbuf_tensor(name, shape, dt))
        ps = lambda name, shape: ctx.enter_context(nc.psum_tensor(name, shape, F32))
        sem = kp["sem"]
        band = sb("band", [128, 4, 128])
        band_hi = sb("band_hi", [128, 4, 128], F32R)
        band_lo = sb("band_lo", [128, 4, 128], F32R)
        cross = sb("cross", [128, 2, 128])
        cross_r = sb("cross_parts", [128, 2, 128], F32R)
        one_img = sb("ones_padded", [128, PADW])
        field = sb("blurred_ones", [128, 2, W])
        y_t = sb("y_tile", [128, 4, 2, GRP, W])
        y_hi = sb("y_hi", [128, 2, 2 * GRP, PADW], F32R)
        y_lo = sb("y_lo", [128, 2, 2 * GRP, PADW], F32R)
        halo = sb("halo", [HALO_P, 2, HCH, W])
        halo_r = sb("halo_parts", [HALO_P, 2, HCH, W], F32R)
        o_t = sb("out_tile", [128, 2, 2, GRP, W])
        st = sb("gn2_columns", [128, 8, B])
        spread = sb("gn2_spread", [128, 2, B, NG])
        yp = [ps(f"blur_psum{i}", [128, GRP, W]) for i in range(4)]

        s_lk = sem("vector_link4")
        s_v = sem("vector_result4")
        s_p = sem("tensor_result4")
        s_rs = sem("rstd_ready4")
        s_set = sem("memsets_done4")
        s_ready = sem("blur_constants_ready")
        s_in = [sem(f"y_loaded{i}") for i in range(4)]
        s_hin = [sem(f"halo_loaded{i}") for i in range(2)]
        s_hhi = sem("halo_hi_ready")
        s_hlo = sem("halo_lo_ready")
        s_hi = sem("y_hi_ready")
        s_lo = sem("y_lo_ready")
        s_mm = sem("blur_half_done")
        s_ev = sem("blur_half_taken")
        s_o = sem("out_half_ready")
        s_st = [sem(f"out_stored{i}") for i in range(2)]

        yv = y_d.rearrange("b c h w -> (b c) h w")
        ov = out.rearrange("b c h w -> (b c) h w")
        block = ctx.enter_context(nc.Block())

        def load(sp, n, slot):
            for t in range(2):
                sp.dma_start(y_t[:, slot, t], yv[bass.ds(n * GRP, GRP), t * 128:(t + 1) * 128, :].rearrange(
                    "c p w -> p c w")).then_inc(s_in[slot], 16)

        def load_halo(sp, q, slot):
            for part in range(3):
                for kw in range(4):
                    lo, hi = max(0, 2 - kw), min(W, W + 2 - kw)
                    p0 = part * Q_STEP + kw * HALO_ROWS
                    sp.dma_start(halo[p0:p0 + HALO_ROWS, slot, :, lo:hi],
                                 yv[bass.ds(q * HCH, HCH), 126:126 + HALO_ROWS, lo + kw - 2:hi + kw - 2].rearrange(
                                     "c p w -> p c w")).then_inc(s_hin[slot], 16)

        @block.sync
        def _(sp):
            for n in range(4):
                load(sp, n, n)
            sp.wait_ge(s_set, 4)
            load_halo(sp, 0, 0)
            load_halo(sp, 1, 1)

            def body(it, last):
                for i in range(BODY4):
                    n = it * BODY4 + i
                    sp.wait_ge(s_o, n * 2 + 2)
                    for t in range(2):
                        sp.dma_start(ov[bass.ds(n * GRP, GRP), t * 128:(t + 1) * 128, :].rearrange("c p w -> p c w"),
                                     o_t[:, i % 2, t]).then_inc(s_st[i % 2], 16)
                    if not (last and i >= 4):
                        load(sp, n + 4, i % 4)
                    if i % 4 == 1 and not last:
                        sp.wait_ge(s_hlo, it * 2 + i // 4 + 1)
                        load_halo(sp, it * 2 + i // 4 + 2, i // 4)

            with sp.Fori(0, LAST) as it:
                body(it, False)
            body(LAST, True)
            for i in range(2):
                sp.wait_ge(s_st[i], 32 + 32 * UNITS4 // 2)

        @block.gpsimd
        def _(pool):
            pool.memset(y_hi[:].bitcast(F32), 0.0).then_inc(s_set, 1)
            pool.memset(y_lo[:].bitcast(F32), 0.0).then_inc(s_set, 1)
            pool.memset(halo[:], 0.0).then_inc(s_set, 1)
            pool.memset(one_img[:], 0.0).then_inc(s_set, 1)
            pool.wait_ge(s_set, 4)
            pool.memset(one_img[:, 2:2 + W], 1.0).then_inc(s_set, 1)
            pool.wait_ge(s_v, 3)
            nc.gpsimd.tensor_tensor(st[:, 6, :], st[:, 5, :], neg_half[:, 0:B], ALU.pow).then_inc(s_rs, 1)

            def halo_rest(q, slot):
                pool.wait_ge(s_hhi, q + 1)
                part = slice(Q_STEP, Q_STEP + 4 * HALO_ROWS)
                nc.gpsimd.tensor_tensor(halo_r[part, slot], halo[part, slot], halo_r[part, slot].bitcast(F32),
                                        ALU.subtract).then_inc(s_hlo, 1)
                pool.wait_ge(s_hlo, q + 1)

            pool.wait_ge(s_rs, 1)
            halo_rest(0, 0)

            def body(it, last):
                for i in range(BODY4):
                    pool.wait_ge(s_hi, it * BODY4 + i + 1)
                    nc.gpsimd.tensor_tensor(
                        y_lo[:, i % 2, :, 2:2 + W], y_t[:, i % 4].rearrange("p t c w -> p (t c) w"),
                        y_hi[:, i % 2, :, 2:2 + W].bitcast(F32), ALU.subtract).then_inc(s_lo, 1)
                    if i % 4 == 2 and not (last and i > 4):
                        pool.wait_ge(s_lo, it * BODY4 + i + 1)
                        halo_rest(it * 2 + i // 4 + 1, (i // 4 + 1) % 2)

            with pool.Fori(0, LAST) as it:
                body(it, False)
            body(LAST, True)

        @block.scalar
        def _(act):
            def split_halo(loaded, slot):
                act.wait_ge(s_hin[slot], loaded)
                nc.scalar.activation(halo_r[:, slot], halo[:, slot], ACT.Copy).then_inc(s_hhi, 1)

            act.wait_ge(s_set, 3)
            split_halo(12 * 16, 0)

            def body(it, last):
                for i in range(BODY4):
                    n = it * BODY4 + i
                    act.wait_ge(s_in[i % 4], it * 64 + 32 * (i // 4 + 1))
                    act.wait_ge(s_mm, n * 2 + 6)
                    nc.scalar.activation(y_hi[:, i % 2, :, 2:2 + W], y_t[:, i % 4].rearrange("p t c w -> p (t c) w"),
                                         ACT.Copy).then_inc(s_hi, 1)
                    if i % 4 == 2 and not (last and i > 4):
                        nxt = i // 4 + 1
                        split_halo((it + nxt // 2 + 1) * (12 * 16), nxt % 2)

            with act.Fori(0, LAST) as it:
                body(it, False)
            body(LAST, True)

        @block.vector
        def _(dve):
            lk = Chain(dve, s_lk)
            NCH = float(HW)
            lk.link(nc.vector.reduce_sum(st[:, 0, :], kp["ll_sum"][:], AX.X))
            lk.link(nc.vector.tensor_tensor(st[:, 1, :], kp["x_cmean"][:], kp["x_gmean"][:], ALU.subtract))
            lk.link(nc.vector.scalar_tensor_tensor(st[:, 2, :], st[:, 0, :], 2.0 / NCH, st[:, 1, :], ALU.mult, ALU.add))
            lk.link(nc.vector.reduce_sum(st[:, 4, :], kp["y_sq"][:], AX.X))
            nc.vector.tensor_scalar(st[:, 3, :], st[:, 4, :], 1.0 / NCH, None, ALU.mult).then_inc(s_v, 2)
            dve.wait_ge(s_p, 1)
            small = yp[0][:].rearrange("p c w -> p (c w)")
            lk.link(nc.vector.tensor_copy(st[:, 4, :], small[:, 0:B]))
            lk.link(nc.vector.tensor_tensor(st[:, 7, :], st[:, 4, :], st[:, 4, :], ALU.mult))
            lk.link(nc.vector.tensor_tensor(st[:, 5, :], small[:, B:2 * B], st[:, 7, :], ALU.subtract))
            nc.vector.tensor_scalar(st[:, 5, :], st[:, 5, :], EPS, None, ALU.add).then_inc(s_v, 1)
            lk.link(nc.vector.tensor_tensor(st[:, 7, :], st[:, 4, :], kp["x_gmean"][:], ALU.add))
            lk.link(nc.vector.tensor_scalar(st[:, 7, :], st[:, 7, :], -1.0, None, ALU.mult))
            dve.wait_ge(s_rs, 1)
            for b in range(B):
                for j, col in enumerate((7, 6)):
                    ins = nc.vector.tensor_scalar(spread[:, j, b, :], K[:, K_GM:K_GM + NG], st[:, col, b:b + 1],
                                                  None, ALU.mult)
            ins.then_inc(s_v, 1)
            dve.wait_ge(s_p, 2)
            lk.link(nc.vector.tensor_copy(nm_b[:].rearrange("p b g -> p (b g)"), small[:, 512:512 + B * NG]))
            lk.link(nc.vector.tensor_copy(rs_b[:].rearrange("p b g -> p (b g)"), small[:, 512 + B * NG:512 + 2 * B * NG]))
            for kw in range(4):
                for kh in range(4):
                    mask = K[:, K_TM + kh * 128:K_TM + (kh + 1) * 128]
                    scalar = kp["KR"][:, kh * 4 + kw:kh * 4 + kw + 1]
                    if kh == 0:
                        lk.link(nc.vector.tensor_scalar(band[:, kw, :], mask, scalar, None, ALU.mult))
                    else:
                        lk.link(nc.vector.scalar_tensor_tensor(band[:, kw, :], mask, scalar, band[:, kw, :],
                                                               ALU.mult, ALU.add))
            for t in range(2):
                for kh in range(4):
                    mask = K[:, K_HM + (t * 4 + kh) * 128:K_HM + (t * 4 + kh + 1) * 128]
                    scalar = kp["HK"][:, kh:kh + 1]
                    if kh == 0:
                        lk.link(nc.vector.tensor_scalar(cross[:, t, :], mask, scalar, None, ALU.mult))
                    else:
                        lk.link(nc.vector.scalar_tensor_tensor(cross[:, t, :], mask, scalar, cross[:, t, :],
                                                               ALU.mult, ALU.add))
            lk.link(nc.vector.tensor_copy(band_hi[:], band[:]))
            lk.link(nc.vector.tensor_tensor(band_lo[:], band[:], band_hi[:].bitcast(F32), ALU.subtract))
            lk.link(nc.vector.tensor_copy(cross_r[:], cross[:]))
            third = slice(2 * Q_STEP, 3 * Q_STEP)
            nc.vector.tensor_tensor(cross_r[third], cross[third], cross_r[third].bitcast(F32),
                                    ALU.subtract).then_inc(s_v, 1)
            dve.wait_ge(s_p, 3)
            for t in range(2):
                ins = nc.vector.tensor_copy(field[:, t, :], yp[1 + t][:, 0, :])
            ins.then_inc(s_ready, 1)
            dve.wait_ge(s_ready, 1)
            for i in range(2):
                dve.sem_inc(s_st[i], 32)

            def body(it, last):
                for i in range(BODY4):
                    n = it * BODY4 + i
                    col = n
                    for t in range(2):
                        dve.wait_ge(s_mm, n * 2 + t + 9)
                        if t == 0:
                            dve.wait_ge(s_st[i % 2], it * (32 * BODY4 // 2) + 32 * (i // 2 + 1))
                        res = o_t[:, i % 2, t]
                        nc.vector.scalar_tensor_tensor(
                            res, field[:, t:t + 1, :].to_broadcast([128, GRP, W]),
                            nm_b[:].rearrange("p b g -> p (b g)")[:, bass.ds(col, 1)],
                            yp[2 * (i % 2) + t][:], ALU.mult, ALU.add).then_inc(s_ev, 1)
                        dve.wait_ge(s_ev, n * 2 + t + 5)
                        nc.vector.scalar_tensor_tensor(
                            res, res, rs_b[:].rearrange("p b g -> p (b g)")[:, bass.ds(col, 1)],
                            y_t[:, i % 4, t], ALU.mult, ALU.add).then_inc(s_o, 1)

            with dve.Fori(0, LAST) as it:
                body(it, False)
            body(LAST, True)

        @block.tensor
        def _(pe):
            pe.sem_inc(s_mm, 8)
            small = yp[0][:].rearrange("p c w -> p (c w)")
            pe.wait_ge(s_v, 2)
            nc.tensor.matmul(small[:, 0:2 * B], K[:, K_G4:K_G4 + C], st[:, 2:4, :].rearrange("p a b -> p (a b)"),
                             start=True, stop=True).then_inc(s_p, 1)
            pe.wait_ge(s_v, 4)
            nc.tensor.matmul(small[:, 512:512 + 2 * B * NG], kp["quarter"][:], spread[:].rearrange("p j b g -> p (j b g)"),
                             start=True, stop=True).then_inc(s_p, 1)
            pe.wait_ge(s_v, 5)
            pe.wait_ge(s_set, 5)
            for t in range(2):
                for kw in range(4):
                    nc.tensor.matmul(yp[1 + t][:, 0, :], band[:, kw, :], one_img[:, kw:kw + W],
                                     start=(kw == 0), stop=False)
                ins = nc.tensor.matmul(yp[1 + t][:, 0, :], cross[0:4 * HALO_ROWS, t, :],
                                       K[0:4 * HALO_ROWS, K_H1:K_H1 + W], start=False, stop=True)
            ins.then_inc(s_p, 1)
            pe.sem_inc(s_ev, 4)
            pe.wait_ge(s_ready, 1)

            def body(it, last):
                for i in range(BODY4):
                    n = it * BODY4 + i
                    pe.wait_ge(s_lo, n + 1)
                    if i % 4 == 0:
                        pe.wait_ge(s_hlo, it * 2 + i // 4 + 1)
                    for t in range(2):
                        pe.wait_ge(s_ev, n * 2 + t + 1)
                        dst = [yp[2 * (i % 2) + t][:, 2 * c:2 * c + 2, :] for c in range(2)]
                        src = lambda y, c, kw: y[:, i % 2, t * GRP + 2 * c:t * GRP + 2 * c + 2, kw:kw + W]
                        for kw in range(4):
                            for wt, y in ((band_hi, y_hi), (band_hi, y_lo), (band_lo, y_hi)):
                                for c in range(2):
                                    nc.tensor.matmul(dst[c], wt[:, kw, :], src(y, c, kw),
                                                     start=(kw == 0 and wt is band_hi and y is y_hi), stop=False)
                        for c in range(2):
                            ch = (i % 4) * GRP + 2 * c
                            ins = nc.tensor.matmul(dst[c], cross_r[0:HALO_P, t, :],
                                                   halo_r[:, i // 4, ch:ch + 2, :], start=False, stop=True)
                        ins.then_inc(s_mm, 1)

            with pe.Fori(0, LAST) as it:
                body(it, False)
            body(LAST, True)


def kernel(x, L0_conv_w_c1, L0_conv_b_c1, L0_conv_bn1_g, L0_conv_bn1_b, L0_conv_dw_w, L0_conv_dw_b,
           L0_conv_gn_g, L0_conv_gn_b, L0_conv_pw1_w, L0_conv_pw1_b, L0_conv_pw2_w, L0_conv_pw2_b,
           L0_conv_w_c2, L0_conv_b_c2, L0_conv_bn2_g, L0_conv_bn2_b, L1_conv_kernel):
    import concourse.bacc as bacc
    from concourse.bass_utils import run_bass_kernel_spmd

    def a(v):
        return np.asarray(v)

    def halo_taps():
        taps = a(L1_conv_kernel)[::-1, ::-1]
        rows = np.zeros((128, 4), np.float32)
        for q in range(3):
            for kw in range(4):
                for r in range(HALO_ROWS):
                    rows[q * Q_STEP + kw * HALO_ROWS + r] = taps[:, kw]
        return rows

    vec = np.concatenate(
        [np.stack([a(v) for v in (L0_conv_b_c1, L0_conv_bn1_g, L0_conv_bn1_b, L0_conv_dw_b, L0_conv_gn_g,
                                  L0_conv_gn_b, L0_conv_pw1_b, L0_conv_pw2_b)], axis=1)]
        + [a(v).reshape(4, C).T for v in (L0_conv_b_c2, L0_conv_bn2_g, L0_conv_bn2_b)]
        + [a(L0_conv_dw_w).reshape(C, TAPS)], axis=1)
    arrays = {
        "x": a(x),
        "vec": vec,
        "wc1": a(L0_conv_w_c1).reshape(C, 4, C).transpose(2, 1, 0),
        "pw1": a(L0_conv_pw1_w).T,
        "pw2": a(L0_conv_pw2_w).T,
        "wc2": a(L0_conv_w_c2).T,
        "kern": np.broadcast_to(a(L1_conv_kernel)[::-1, ::-1].reshape(1, 16), (128, 16)),
        "halo_k": halo_taps(),
        "const": shape_constants(),
    }
    arrays = {k: np.ascontiguousarray(v) for k, v in arrays.items()}
    nc = bacc.Bacc("TRN2", target_bir_lowering=False, num_devices=1)
    args = [nc.dram_tensor(k, v.shape, mybir.dt.from_np(v.dtype), kind="ExternalInput").ap()
            for k, v in arrays.items()]
    out = nc.dram_tensor("out", (B, C, H, W), F32, kind="ExternalOutput").ap()
    build(nc, *args, out)
    r = run_bass_kernel_spmd(nc, [arrays], core_ids=[0])
    return r.results[0]["out"]
```

```python
import numpy as np
import concourse.bass as bass
from concourse import mybir
from contextlib import ExitStack

F32 = mybir.dt.float32
F32R = mybir.dt.float32r
BF16 = mybir.dt.bfloat16
ALU = mybir.AluOpType
ACT = mybir.ActivationFunctionType
AX = mybir.AxisListType

B, C, H, W = 8, 128, 256, 256
HW = H * W
H2, W2 = H // 2, W // 2
HW2 = H2 * W2
GRP = 4
NG = C // GRP
EPS = 1e-5
BANK = 512
TAPS = 9
BN_W = 6

V_BC1, V_BN1G, V_BN1B, V_DWB, V_GNG, V_GNB, V_PW1B, V_PW2B = range(8)
V_BC2, V_BN2G, V_BN2B, V_DWW = 8, 12, 16, 20
V_ALL = V_DWW + TAPS

K_ID = 0
K_G4 = K_ID + C
K_GM = K_G4 + C
K_TM = K_GM + NG
K_HM = K_TM + 4 * 128
K_H1 = K_HM + 2 * 4 * 128
K_ALL = K_H1 + W

HALO_ROWS = 3
Q_STEP = 32
HALO_P = 2 * Q_STEP + 4 * HALO_ROWS


def shape_constants():
    k = np.zeros((128, K_ALL), np.float32)
    k[:, K_ID:K_ID + C] = np.eye(C)
    p = np.arange(128)
    k[:, K_G4:K_G4 + C] = (p[:, None] // GRP == p[None, :] // GRP) / GRP
    k[:, K_GM:K_GM + NG] = p[:, None] // GRP == np.arange(NG)[None, :]
    for kh in range(4):
        k[:, K_TM + kh * 128:K_TM + (kh + 1) * 128] = p[:, None] - p[None, :] == kh - 2
    for q in range(3):
        for kw in range(4):
            for r in range(HALO_ROWS):
                row = q * Q_STEP + kw * HALO_ROWS + r
                for t in range(2):
                    for m in ((127,), (0, 1))[t]:
                        kh = 126 + r - (128 * t + m) + 2
                        if 0 <= kh < 4 and (r == 2) == (t == 0):
                            k[row, K_HM + (t * 4 + kh) * 128 + m] = 1.0
                w = np.arange(W) + kw - 2
                k[row, K_H1:K_H1 + W] = (w >= 0) & (w < W)
    return k


class Chain:

    def __init__(self, engine, semaphore, base=0):
        self.engine, self.semaphore, self.base, self.n = engine, semaphore, base, 0

    def link(self, instruction):
        self.n += 1
        instruction.then_inc(self.semaphore, 1)
        self.engine.wait_ge(self.semaphore, self.base + self.n)


def build(nc, x, vec, wc1, pw1, pw2, wc2, kern, halo_k, const, out):
    z_d = nc.dram_tensor("z_scratch", (C, B, HW2), F32, kind="Internal").ap()
    u_d = nc.dram_tensor("u_scratch", (C, B, HW2), F32, kind="Internal").ap()
    y_d = nc.dram_tensor("y_scratch", (B, C, H, W), F32, kind="Internal").ap()
    with ExitStack() as keep:
        def sbk(name, shape, dt=F32):
            return keep.enter_context(nc.sbuf_tensor(name, shape, dt))

        K = sbk("constants", [128, K_ALL])
        V = sbk("vectors", [128, V_ALL])
        KR = sbk("blur_taps", [128, 16])
        HK = sbk("blur_halo_taps", [128, 4])
        neg_half = sbk("neg_half", [128, NG])
        n128 = sbk("mean_over_channels", [128, 128])
        quarter = sbk("quarter", [128, 128])
        x_gmean = sbk("x_group_mean", [128, B])
        x_cmean = sbk("x_channel_mean", [128, B])
        z_sum = sbk("z_sum", [128, B * CH1])
        z_sq = sbk("z_sq", [128, B * CH1])
        gram = sbk("gram", [128, C + 1])
        bn2_a = sbk("bn2_scale", [128, 4])
        bn2_d = sbk("bn2_shift", [128, 4])
        ll_sum = sbk("ll_sum", [128, B, 32])
        y_sq = sbk("y_sq", [128, B, 32])
        nm_b = sbk("neg_mean_all", [128, B, NG])
        rs_b = sbk("rstd_all", [128, B, NG])
        sem = lambda name: keep.enter_context(nc.semaphore(name))
        keepers = dict(sem=sem, K=K, V=V, KR=KR, HK=HK, neg_half=neg_half, n128=n128, quarter=quarter,
                       x_gmean=x_gmean, x_cmean=x_cmean, z_sum=z_sum, z_sq=z_sq, gram=gram,
                       bn2_a=bn2_a, bn2_d=bn2_d, ll_sum=ll_sum, y_sq=y_sq, nm_b=nm_b, rs_b=rs_b)
        phase_conv1(nc, keepers, x, vec, wc1, kern, halo_k, const, z_d)
        phase_mix(nc, keepers, pw1, pw2, z_d, u_d)
        phase_conv2(nc, keepers, wc2, x, u_d, y_d)
        phase_blur(nc, keepers, y_d, out)


ROWS1 = 8
CH1 = H // ROWS1
NS = 22
AGAIN = 12
LOADS = CH1 + AGAIN
ZP = 6
LINKS1 = 5


def conv_position(load):
    return load - AGAIN


def phase_conv1(nc, kp, x, vec, wc1, kern, halo_k, const, z_d):
    K, V, n128 = kp["K"], kp["V"], kp["n128"]
    CW = ROWS1 * W
    ZW = CW // 4
    with ExitStack() as ctx:
        sb = lambda name, shape, dt=F32: ctx.enter_context(nc.sbuf_tensor(name, shape, dt))
        ps = lambda name, shape: ctx.enter_context(nc.psum_tensor(name, shape, F32))
        sem = kp["sem"]
        ring = sb("x_ring", [128, NS, CW])
        stats = sb("x_stats", [128, CH1 * CW // BANK, BN_W])
        w_ph = sb("w_phase", [128, 4, C])
        w_f = sb("w_folded", [128, 4, C])
        zt = sb("z_tile", [128, 2, ZW])
        w_sub = zt[:, 0, 0:4 * C].rearrange("p (s o) -> p s o", o=C)
        t_ab = zt[:, 1, 0:4 * C].rearrange("p (s o) -> p s o", o=C)
        mv = sb("x_mean_var", [128, 2])
        waiter = sb("waiter1", [128, 1])
        d = sb("x_dev", [128, 1])
        ve = sb("x_var_eps", [128, 1])
        rs = sb("x_rstd", [128, 1])
        negb = sb("group_mean_now", [128, 1])
        bias = sb("z_bias", [128, 1])
        zp = [ps(f"z_psum{i}", [128, ZW]) for i in range(ZP)]
        small = ps("small1", [128, 4])

        s_const = sem("const_loaded")
        s_set = sem("memsets_done")
        s_prep = sem("phase_weights_done")
        s_x = [sem(f"x_loaded{i}") for i in range(NS)]
        s_stat = sem("x_chunk_counted")
        s_conv = sem("x_chunk_convolved")
        s_link = sem("vector_link1")
        s_mv = sem("channel_stats_ready")
        s_avg = sem("group_average_ready")
        s_ve = sem("variance_ready")
        s_rs = sem("rstd_ready")
        s_fold = sem("weights_folded")
        s_bmm = sem("bias_product_ready")
        s_bias = sem("bias_ready")
        s_evac = sem("z_evacuated")
        s_sq = sem("z_squared")
        s_zst = [sem(f"z_stored{i}") for i in range(2)]

        xv = x.rearrange("b c h w -> b c (h w)")
        block = ctx.enter_context(nc.Block())

        def chunk_of(load):
            return load if load < CH1 else load - CH1

        @block.sync
        def _(sp):
            n = 0
            for dst, src in ((K[:], const), (V[:], vec), (w_sub, wc1), (kp["KR"][:], kern),
                             (kp["HK"][:], halo_k)):
                sp.dma_start(dst, src).then_inc(s_const, 16)
            with sp.Fori(0, B) as b:
                for load in range(LOADS):
                    before = load - NS
                    if 0 <= before < AGAIN:
                        sp.wait_ge(s_stat, b * CH1 + before + 1)
                    elif before >= 0:
                        sp.wait_ge(s_conv, b * CH1 + CH1 + conv_position(before) + 1)
                    else:
                        sp.wait_ge(s_conv, b * CH1 + conv_position(load + NS) + 1)
                    c0 = chunk_of(load) * CW
                    sp.dma_start(ring[:, load % NS, :],
                                 xv[bass.ds(b, 1), :, c0:c0 + CW].rearrange("b c n -> c (b n)")
                                 ).then_inc(s_x[load % NS], 16)

        @block.gpsimd
        def _(pool):
            pool.memset(kp["neg_half"][:], -0.5).then_inc(s_set, 1)
            pool.memset(n128[:], 1.0 / C).then_inc(s_set, 1)
            pool.memset(kp["quarter"][:], 1.0 / GRP).then_inc(s_set, 1)
            pool.wait_ge(s_set, 3)
            with pool.Fori(0, B) as b:
                pool.wait_ge(s_ve, b + 1)
                nc.gpsimd.tensor_tensor(rs[:], ve[:], kp["neg_half"][:, 0:1], ALU.pow).then_inc(s_rs, 1)

        @block.vector
        def _(dve):
            dve.wait_ge(s_const, 16 * 5)
            pair = w_sub.rearrange("p (a b) o -> p a b o", b=2)
            nc.vector.tensor_tensor(t_ab[:, 0:2, :], pair[:, :, 0, :], pair[:, :, 1, :], ALU.add).then_inc(s_prep, 1)
            nc.vector.tensor_tensor(t_ab[:, 2:4, :], pair[:, :, 0, :], pair[:, :, 1, :], ALU.subtract).then_inc(s_prep, 1)
            dve.wait_ge(s_prep, 2)
            tp = t_ab.rearrange("p (a b) o -> p a b o", b=2)
            wp = w_ph[:].rearrange("p (a b) o -> p a b o", b=2)
            nc.vector.tensor_tensor(wp[:, :, 0, :], tp[:, :, 0, :], tp[:, :, 1, :], ALU.add).then_inc(s_prep, 1)
            nc.vector.tensor_tensor(wp[:, :, 1, :], tp[:, :, 0, :], tp[:, :, 1, :], ALU.subtract).then_inc(s_prep, 1)
            dve.wait_ge(s_prep, 4)
            nc.vector.tensor_scalar(w_ph[:], w_ph[:], 0.5, None, ALU.mult).then_inc(s_prep, 1)
            dve.wait_ge(s_prep, 5)
            with dve.Fori(0, B) as b:
                for c in range(CH1):
                    dve.wait_ge(s_x[c % NS], b * 32 + 16 * (c // NS + 1))
                    for k in range(CW // BANK):
                        ins = nc.vector.bn_stats(stats[:, c * (CW // BANK) + k, :],
                                                 ring[:, c % NS, k * BANK:(k + 1) * BANK])
                    ins.then_inc(s_stat, 1)
                dve.wait_ge(s_stat, b * CH1 + CH1)
                nc.vector.memset(waiter[:], 0.0)
                nc.vector.bn_aggr(mv[:], stats[:].rearrange("p a b -> p (a b)")).then_inc(s_mv, 1)
                dve.wait_ge(s_mv, b * 2 + 1)
                ch = Chain(dve, s_link, b * LINKS1)
                dve.wait_ge(s_avg, b * 2 + 1)
                ch.link(nc.vector.tensor_copy(kp["x_gmean"][:, bass.ds(b, 1)], small[:, 0:1]))
                ch.link(nc.vector.tensor_copy(kp["x_cmean"][:, bass.ds(b, 1)], mv[:, 0:1]))
                ch.link(nc.vector.tensor_tensor(d[:], mv[:, 0:1], small[:, 0:1], ALU.subtract))
                ch.link(nc.vector.scalar_tensor_tensor(d[:], d[:], d[:], mv[:, 1:2], ALU.mult, ALU.add))
                ch.link(nc.vector.tensor_copy(negb[:], small[:, 0:1]))
                nc.vector.tensor_copy(mv[:, 1:2], d[:]).then_inc(s_mv, 1)
                dve.wait_ge(s_avg, b * 2 + 2)
                nc.vector.tensor_scalar(ve[:], small[:, 1:2], EPS, None, ALU.add).then_inc(s_ve, 1)
                dve.wait_ge(s_rs, b + 1)
                nc.vector.tensor_scalar(w_f[:], w_ph[:], rs[:], None, ALU.mult).then_inc(s_fold, 1)
                dve.wait_ge(s_bmm, b + 1)
                dve.wait_ge(s_sq, b * CH1 + ZP)
                nc.vector.tensor_scalar(bias[:], small[:, 2:3], -1.0, None, ALU.mult).then_inc(s_bias, 1)
                assert ch.n == LINKS1

        @block.tensor
        def _(pe):
            pe.sem_inc(s_conv, CH1)
            pe.wait_ge(s_const, 16 * 5)
            pe.wait_ge(s_set, 3)
            with pe.Fori(0, B) as b:
                pe.wait_ge(s_mv, b * 2 + 1)
                nc.tensor.matmul(small[:, 0:1], K[:, K_G4:K_G4 + C], mv[:, 0:1], start=True, stop=True).then_inc(s_avg, 1)
                pe.wait_ge(s_mv, b * 2 + 2)
                nc.tensor.matmul(small[:, 1:2], K[:, K_G4:K_G4 + C], mv[:, 1:2], start=True, stop=True).then_inc(s_avg, 1)
                pe.wait_ge(s_fold, b + 1)
                for p in range(4):
                    ins = nc.tensor.matmul(small[:, 2:3], w_f[:, p, :], negb[:], start=(p == 0), stop=(p == 3))
                ins.then_inc(s_bmm, 1)
                for q in range(CH1):
                    load = q + AGAIN
                    pe.wait_ge(s_x[load % NS], b * 32 + 16 * (load // NS + 1))
                    pe.wait_ge(s_sq, b * CH1 + max(q, ZP - 1) + 1)
                    px = ring[:, load % NS, :].rearrange("c (i a j e) -> c a e i j", a=2, e=2, j=W2)
                    for half in range(ZW // BANK):
                        rows = slice(half * 4, half * 4 + 4)
                        for p in range(4):
                            ins = nc.tensor.matmul(zp[q % ZP][:, half * BANK:(half + 1) * BANK],
                                                   w_f[:, p, :], px[:, p // 2, p % 2, rows, :],
                                                   start=(p == 0), stop=(p == 3))
                    ins.then_inc(s_conv, 1)

        @block.scalar
        def _(act):
            zv = z_d.rearrange("c b n -> b c n")
            act.sem_inc(s_sq, ZP)
            for i in range(2):
                act.sem_inc(s_zst[i], 16)
            with act.Fori(0, B) as b:
                act.wait_ge(s_bias, b + 1)
                for q in range(CH1):
                    act.wait_ge(s_conv, b * CH1 + CH1 + q + 1)
                    act.wait_ge(s_zst[q % 2], b * 16 * (CH1 // 2) + 16 * (q // 2 + 1))
                    nc.scalar.activation(zt[:, q % 2, :], zp[q % ZP][:], ACT.Identity, bias=bias[:],
                                         accum_out=kp["z_sum"][:, bass.ds(b * CH1 + q, 1)]).then_inc(s_evac, 1)
                    act.wait_ge(s_evac, b * CH1 + q + 1)
                    nc.scalar.activation(zp[q % ZP][:], zp[q % ZP][:], ACT.Square, bias=bias[:],
                                         accum_out=kp["z_sq"][:, bass.ds(b * CH1 + q, 1)]).then_inc(s_sq, 1)
                    chunk = chunk_of(q + AGAIN)
                    act.dma_start(zv[bass.ds(b, 1), :, chunk * ZW:(chunk + 1) * ZW].rearrange("b c n -> c (b n)"),
                                  zt[:, q % 2, :]).then_inc(s_zst[q % 2], 16)
            for i in range(2):
                act.wait_ge(s_zst[i], 16 + 16 * B * CH1 // 2)


R2 = BANK // W2
STEPS = H2 // R2
PE_TAPS = 3
LINKS_LN = 5
LAG_Z = 1
LAG_TR = 1
LAG_EVAC = 2
LAG_GRAM = 3
LAG_DW = 3
LAG_TAPS = 4
LAG_LAST = 3
LAG_STATS = 5
AHEAD = 2


def phase_mix(nc, kp, pw1, pw2, z_d, u_d):
    K, V, n128, neg_half = kp["K"], kp["V"], kp["n128"], kp["neg_half"]
    gram = kp["gram"]
    DVE_TAPS = TAPS - PE_TAPS - 1
    with ExitStack() as ctx:
        sb = lambda name, shape, dt=F32: ctx.enter_context(nc.sbuf_tensor(name, shape, dt))
        ps = lambda name, shape: ctx.enter_context(nc.psum_tensor(name, shape, F32))
        sem = kp["sem"]
        plane = sb("h_plane", [128, H2 + 2, W2 + 2])
        o_buf = sb("depthwise_out", [128, STEPS, BANK])
        z_in = sb("z_in", [128, 4, BANK])
        diag = sb("tap_diagonals", [128, PE_TAPS, C])
        w1 = sb("pw1_weights", [128, C])
        w1f = sb("pw1_folded", [128, C])
        w2 = sb("pw2_weights", [128, C])
        v_t = sb("gelu1_out", [128, 2, BANK])
        last_tap = sb("last_tap", [128, 2, BANK])
        u_t = sb("u_tile", [128, 4, BANK])
        u_tr = sb("u_transposed", [128, 2, 4, C + 1])
        bst = sb("o_stats", [128, STEPS, BN_W])
        mv = sb("o_mean_var", [128, 2])
        waiter = sb("waiter2", [128, 1])
        t = sb("small_columns", [128, 8])
        bn1_a = sb("bn1_scale", [128, 1])
        bn1_d = sb("bn1_shift", [128, 1])
        b1 = sb("pw1_bias", [128, 1])
        dw_p = [ps(f"dw_psum{i}", [128, BANK]) for i in range(2)]
        p1_p = [ps(f"pw1_psum{i}", [128, BANK]) for i in range(2)]
        p2_p = ps("pw2_psum", [128, BANK])
        tr_p = [ps(f"transpose_psum{i}", [128, BANK]) for i in range(2)]
        g_p = ps("gram_psum", [128, BANK])
        small = g_p[:, 256:260]

        s_w = sem("pw_weights_loaded")
        s_zero = sem("plane_zeroed")
        s_lk = sem("vector_link2")
        s_lk_tap = sem("tap_link")
        s_lk_ln = sem("layer_norm_link")
        s_pow = sem("pow_wanted2")
        s_rs = sem("rstd_ready2")
        s_bn1 = sem("bn1_ready")
        s_z = [sem(f"z_loaded{i}") for i in range(4)]
        s_h = sem("h_rows_ready")
        s_dw = sem("dw_psum_ready")
        s_lt = sem("last_tap_ready")
        s_oo = sem("depthwise_complete")
        s_o = sem("o_stats_done")
        s_lnm = sem("ln_means_wanted")
        s_lna = sem("ln_average_ready")
        s_ln = sem("pw1_folded_ready")
        s_lnb = sem("pw1_bias_product")
        s_b1 = sem("pw1_bias_ready")
        s_p1 = sem("pw1_ready")
        s_g1 = sem("gelu1_ready")
        s_p2 = sem("pw2_ready")
        s_u = sem("u_ready")
        s_tr = sem("u_transposed_psum")
        s_ut = sem("u_transposed_sbuf")
        s_gm = sem("gram_step_done")
        s_gacc = sem("gram_added")
        s_ust = [sem(f"u_stored{i}") for i in range(4)]

        zv = z_d.rearrange("c b n -> b c n")
        uv = u_d.rearrange("c b n -> b c n")
        block = ctx.enter_context(nc.Block())

        def tap(k, j):
            kh, kw = k // 3, k % 3
            return plane[:, j * R2 + kh:j * R2 + kh + R2, kw:kw + W2]

        def rows_of(j):
            return plane[:, 1 + j * R2:1 + (j + 1) * R2, 1:1 + W2]

        @block.sync
        def _(sp):
            sp.dma_start(w1[:], pw1).then_inc(s_w, 16)
            sp.dma_start(w2[:], pw2).then_inc(s_w, 16)

            def body(b, enters, leaves):
                def load(j):
                    sp.wait_ge(s_h, b * (STEPS + 1) + j + 1)
                    sp.dma_start(z_in[:, j % 4, :],
                                 zv[bass.ds(b, 1), :, j * BANK:(j + 1) * BANK].rearrange("b c n -> c (b n)")
                                 ).then_inc(s_z[j % 4], 16)

                def store(j):
                    sp.wait_ge(s_u, (b - 1) * STEPS + j + 1)
                    sp.dma_start(uv[bass.ds(b - 1, 1), :, j * BANK:(j + 1) * BANK].rearrange("b c n -> c (b n)"),
                                 u_t[:, j % 4, :]).then_inc(s_ust[j % 4], 16)

                for j in range(-AHEAD, STEPS):
                    if enters and j + AHEAD < STEPS:
                        load(j + AHEAD)
                    if leaves and j >= 0:
                        store(j)

            body(0, True, False)
            with sp.Fori(1, B) as b:
                body(b, True, True)
            body(B, False, True)
            for i in range(4):
                sp.wait_ge(s_ust[i], 16 + 16 * B * STEPS // 4)

        @block.gpsimd
        def _(pool):
            pool.memset(plane[:, 0:H2 + 2:H2 + 1, :], 0.0).then_inc(s_zero, 1)
            pool.memset(plane[:, 1:H2 + 1, 0:W2 + 2:W2 + 1], 0.0).then_inc(s_zero, 1)
            pool.memset(u_tr[:, :, :, C:C + 1], 1.0).then_inc(s_zero, 1)
            pool.wait_ge(s_pow, 1)
            nc.gpsimd.tensor_tensor(t[:, 3:4], t[:, 2:3], neg_half[:, 0:1], ALU.pow).then_inc(s_rs, 1)
            with pool.Fori(0, B) as b:
                for j in range(STEPS):
                    pool.wait_ge(s_lk_tap, b * STEPS * DVE_TAPS + (j + 1) * DVE_TAPS)
                    pool.wait_ge(s_lt, b * STEPS + j + 1)
                    nc.gpsimd.tensor_tensor(o_buf[:, j, :], o_buf[:, j, :], last_tap[:, j % 2, :],
                                            ALU.add).then_inc(s_oo, 1)
                pool.wait_ge(s_pow, b + 2)
                nc.gpsimd.tensor_tensor(t[:, 3:4], t[:, 2:3], neg_half[:, 0:1], ALU.pow).then_inc(s_rs, 1)

        @block.vector
        def _(dve):
            N = float(B * HW2)
            lk = Chain(dve, s_lk)
            lk.link(nc.vector.memset(gram[:], 0.0))
            lk.link(nc.vector.reduce_sum(t[:, 0:1], kp["z_sum"][:], AX.X))
            lk.link(nc.vector.reduce_sum(t[:, 1:2], kp["z_sq"][:], AX.X))
            lk.link(nc.vector.tensor_scalar(t[:, 0:2], t[:, 0:2], 1.0 / N, None, ALU.mult))
            lk.link(nc.vector.tensor_tensor(t[:, 4:5], t[:, 0:1], t[:, 0:1], ALU.mult))
            lk.link(nc.vector.tensor_tensor(t[:, 4:5], t[:, 1:2], t[:, 4:5], ALU.subtract))
            nc.vector.tensor_scalar(t[:, 2:3], t[:, 4:5], EPS, None, ALU.add).then_inc(s_pow, 1)
            lk.link(nc.vector.tensor_tensor(t[:, 5:6], t[:, 0:1], V[:, V_BC1:V_BC1 + 1], ALU.add))
            lk.link(nc.vector.tensor_tensor(t[:, 6:7], V[:, V_BC1:V_BC1 + 1], t[:, 5:6], ALU.subtract))
            dve.wait_ge(s_rs, 1)
            lk.link(nc.vector.tensor_tensor(bn1_a[:], t[:, 3:4], V[:, V_BN1G:V_BN1G + 1], ALU.mult))
            nc.vector.scalar_tensor_tensor(bn1_d[:], t[:, 6:7], bn1_a[:], V[:, V_BN1B:V_BN1B + 1],
                                           ALU.mult, ALU.add).then_inc(s_bn1, 1)
            for k in range(PE_TAPS):
                nc.vector.tensor_scalar(diag[:, k, :], K[:, K_ID:K_ID + C], V[:, V_DWW + k:V_DWW + k + 1],
                                        None, ALU.mult).then_inc(s_bn1, 1)
            dve.wait_ge(s_w, 32)
            for i in range(4):
                dve.sem_inc(s_ust[i], 16)

            def layer_norm(b):
                ln = Chain(dve, s_lk_ln, b * LINKS_LN)
                dve.wait_ge(s_o, (b + 1) * STEPS)
                nc.vector.memset(waiter[:], 0.0)
                ln.link(nc.vector.bn_aggr(mv[:], bst[:].rearrange("p a b -> p (a b)")))
                nc.vector.tensor_tensor(t[:, 0:1], mv[:, 0:1], V[:, V_DWB:V_DWB + 1], ALU.add).then_inc(s_lnm, 1)
                dve.wait_ge(s_lna, b * 2 + 1)
                dve.wait_ge(s_lnm, b * 2 + 1)
                ln.link(nc.vector.tensor_tensor(t[:, 4:5], t[:, 0:1], small[:, 0:1], ALU.subtract))
                ln.link(nc.vector.tensor_tensor(t[:, 5:6], V[:, V_DWB:V_DWB + 1], small[:, 0:1], ALU.subtract))
                nc.vector.scalar_tensor_tensor(t[:, 1:2], t[:, 4:5], t[:, 4:5], mv[:, 1:2],
                                               ALU.mult, ALU.add).then_inc(s_lnm, 1)
                dve.wait_ge(s_lna, b * 2 + 2)
                nc.vector.tensor_scalar(t[:, 2:3], small[:, 1:2], EPS, None, ALU.add).then_inc(s_pow, 1)
                dve.wait_ge(s_rs, b + 2)
                ln.link(nc.vector.tensor_tensor(t[:, 6:7], t[:, 3:4], V[:, V_GNG:V_GNG + 1], ALU.mult))
                ln.link(nc.vector.tensor_scalar(w1f[:], w1[:], t[:, 6:7], None, ALU.mult))
                nc.vector.scalar_tensor_tensor(t[:, 7:8], t[:, 5:6], t[:, 6:7], V[:, V_GNB:V_GNB + 1],
                                               ALU.mult, ALU.add).then_inc(s_ln, 1)
                dve.wait_ge(s_lnb, b + 1)
                nc.vector.tensor_tensor(b1[:], small[:, 2:3], V[:, V_PW1B:V_PW1B + 1], ALU.add).then_inc(s_b1, 1)
                assert ln.n == LINKS_LN

            def body(b, enters, leaves):
                taps = Chain(dve, s_lk_tap, b * STEPS * DVE_TAPS)

                def residual(j):
                    dve.wait_ge(s_p2, (b - 1) * STEPS + j + 1)
                    dve.wait_ge(s_ust[j % 4], (b - 1) * 16 * (STEPS // 4) + 16 * (j // 4 + 1))
                    if j >= 4:
                        dve.wait_ge(s_tr, (b - 1) * STEPS + j - 3)
                    nc.vector.scalar_tensor_tensor(
                        u_t[:, j % 4, :].rearrange("p (r c) -> p r c", c=W2),
                        p2_p[:].rearrange("p (r c) -> p r c", c=W2), V[:, V_PW2B:V_PW2B + 1],
                        rows_of(j), ALU.add, ALU.add).then_inc(s_u, 1)

                def depthwise(j):
                    dve.wait_ge(s_dw, b * STEPS + j + 1)
                    for n, k in enumerate(range(PE_TAPS, TAPS - 1)):
                        taps.link(nc.vector.scalar_tensor_tensor(
                            o_buf[:, j, :].rearrange("p (r c) -> p r c", c=W2), tap(k, j),
                            V[:, V_DWW + k:V_DWW + k + 1],
                            (dw_p[j % 2][:] if n == 0 else o_buf[:, j, :]).rearrange("p (r c) -> p r c", c=W2),
                            ALU.mult, ALU.add))

                def statistics(j):
                    dve.wait_ge(s_oo, b * STEPS + j + 1)
                    nc.vector.bn_stats(bst[:, j, :], o_buf[:, j, :]).then_inc(s_o, 1)

                for j in range(STEPS + LAG_STATS):
                    if leaves and j < STEPS:
                        residual(j)
                    if enters and LAG_TAPS <= j < STEPS + LAG_TAPS:
                        depthwise(j - LAG_TAPS)
                    if enters and j >= LAG_STATS:
                        statistics(j - LAG_STATS)
                if leaves:
                    dve.wait_ge(s_gm, b * STEPS)
                    nc.vector.tensor_tensor(gram[:], gram[:], g_p[:, 0:C + 1], ALU.add).then_inc(s_gacc, 1)
                    dve.wait_ge(s_gacc, b)
                if enters:
                    layer_norm(b)

            body(0, True, False)
            with dve.Fori(1, B) as b:
                body(b, True, True)
            body(B, False, True)

        @block.tensor
        def _(pe):
            pe.wait_ge(s_bn1, 1 + PE_TAPS)
            pe.wait_ge(s_w, 32)
            pe.wait_ge(s_zero, 3)

            def body(b, enters, leaves):
                c = b - 1

                def taps_step(j):
                    pe.wait_ge(s_h, 4 + b * (STEPS + 1) + j + 2)
                    if j >= 2:
                        pe.wait_ge(s_lk_tap, b * STEPS * DVE_TAPS + (j - 2) * DVE_TAPS + 1)
                    for k in range(PE_TAPS):
                        ins = nc.tensor.matmul(dw_p[j % 2][:], diag[:, k, :], tap(k, j),
                                               start=(k == 0), stop=(k == PE_TAPS - 1))
                    ins.then_inc(s_dw, 1)

                def pw1_step(j):
                    if j >= 2:
                        pe.wait_ge(s_g1, c * STEPS + j - 1)
                    nc.tensor.matmul(p1_p[j % 2][:], w1f[:], o_buf[:, j, :], start=True, stop=True).then_inc(s_p1, 1)

                def pw2_step(j):
                    pe.wait_ge(s_g1, c * STEPS + j + 1)
                    if j >= 1:
                        pe.wait_ge(s_u, c * STEPS + j)
                    nc.tensor.matmul(p2_p[:], w2[:], v_t[:, j % 2, :], start=True, stop=True).then_inc(s_p2, 1)

                def transpose_step(j):
                    pe.wait_ge(s_u, c * STEPS + j + 1)
                    if j >= 2:
                        pe.wait_ge(s_ut, c * STEPS + j - 1)
                    for q in range(4):
                        ins = nc.tensor.transpose(tr_p[j % 2][:, q * C:(q + 1) * C],
                                                  u_t[:, j % 4, q * C:(q + 1) * C], K[:, K_ID:K_ID + C])
                    ins.then_inc(s_tr, 1)

                def gram_step(j):
                    pe.wait_ge(s_ut, c * STEPS + j + 1)
                    for q in range(4):
                        ins = nc.tensor.matmul(g_p[:, 0:C + 1], u_tr[:, j % 2, q, 0:C], u_tr[:, j % 2, q, :],
                                               start=(j == 0 and q == 0), stop=(j == STEPS - 1 and q == 3))
                    ins.then_inc(s_gm, 1)

                if leaves:
                    pe.wait_ge(s_b1, b)
                    pw1_step(0)
                for j in range(STEPS + LAG_DW):
                    if leaves and j + 1 < STEPS:
                        pw1_step(j + 1)
                    if leaves and j < STEPS:
                        pw2_step(j)
                    if enters and j >= LAG_DW:
                        taps_step(j - LAG_DW)
                    if leaves and LAG_TR <= j < STEPS + LAG_TR:
                        transpose_step(j - LAG_TR)
                    if leaves and j >= LAG_GRAM:
                        gram_step(j - LAG_GRAM)
                if enters:
                    pe.wait_ge(s_lnm, b * 2 + 1)
                    nc.tensor.matmul(small[:, 0:1], n128[:], t[:, 0:1], start=True, stop=True).then_inc(s_lna, 1)
                    pe.wait_ge(s_lnm, b * 2 + 2)
                    nc.tensor.matmul(small[:, 1:2], n128[:], t[:, 1:2], start=True, stop=True).then_inc(s_lna, 1)
                    pe.wait_ge(s_ln, b + 1)
                    nc.tensor.matmul(small[:, 2:3], w1[:], t[:, 7:8], start=True, stop=True).then_inc(s_lnb, 1)

            body(0, True, False)
            with pe.Fori(1, B) as b:
                body(b, True, True)
            body(B, False, True)

        @block.scalar
        def _(act):
            act.sem_inc(s_h, 4)
            act.wait_ge(s_bn1, 1)
            act.wait_ge(s_zero, 3)

            def body(b, enters, leaves):
                c = b - 1

                def gelu_first(j):
                    act.wait_ge(s_z[j % 4], b * 16 * (STEPS // 4) + 16 * (j // 4 + 1))
                    if leaves:
                        act.wait_ge(s_u, c * STEPS + j + 1)
                    nc.scalar.activation(rows_of(j), z_in[:, j % 4, :].rearrange("p (r c) -> p r c", c=W2),
                                         ACT.Gelu, scale=bn1_a[:], bias=bn1_d[:]).then_inc(s_h, 1)

                def gelu_second(j):
                    act.wait_ge(s_p1, c * STEPS + j + 1)
                    if j >= 2:
                        act.wait_ge(s_p2, c * STEPS + j - 1)
                    nc.scalar.activation(v_t[:, j % 2, :], p1_p[j % 2][:], ACT.Gelu, bias=b1[:]).then_inc(s_g1, 1)

                def evacuate(j):
                    act.wait_ge(s_tr, c * STEPS + j + 1)
                    if j >= 2:
                        act.wait_ge(s_gm, c * STEPS + j - 1)
                    nc.scalar.activation(u_tr[:, j % 2, :, 0:C], tr_p[j % 2][:].rearrange("p (q c) -> p q c", c=C),
                                         ACT.Copy).then_inc(s_ut, 1)

                def tap_last(j):
                    act.wait_ge(s_h, 4 + b * (STEPS + 1) + j + 2)
                    if j >= 2:
                        act.wait_ge(s_oo, b * STEPS + j - 1)
                    nc.scalar.activation(last_tap[:, j % 2, :].rearrange("p (r c) -> p r c", c=W2), tap(TAPS - 1, j),
                                         ACT.Copy, scale=V[:, V_DWW + TAPS - 1:V_DWW + TAPS]).then_inc(s_lt, 1)

                if leaves:
                    act.wait_ge(s_b1, b)
                for j in range(STEPS + LAG_LAST):
                    if leaves and j < STEPS:
                        gelu_second(j)
                    if enters and LAG_Z <= j < STEPS + LAG_Z:
                        gelu_first(j - LAG_Z)
                        if j == STEPS:
                            act.wait_ge(s_h, 4 + b * (STEPS + 1) + STEPS)
                            act.sem_inc(s_h, 1)
                    if leaves and LAG_EVAC <= j < STEPS + LAG_EVAC:
                        evacuate(j - LAG_EVAC)
                    if enters and j >= LAG_LAST:
                        tap_last(j - LAG_LAST)

            body(0, True, False)
            with act.Fori(1, B) as b:
                body(b, True, True)
            body(B, False, True)


ROWS3 = 8
UNITS3 = H // ROWS3
UW = ROWS3 * W // 4
XS = 8
US = 8
GS = 4
LAG_SQ = 3


def phase_conv2(nc, kp, wc2, x, u_d, y_d):
    K, V, neg_half, gram = kp["K"], kp["V"], kp["neg_half"], kp["gram"]
    bn2_a, bn2_d = kp["bn2_a"], kp["bn2_d"]
    with ExitStack() as ctx:
        sb = lambda name, shape, dt=F32: ctx.enter_context(nc.sbuf_tensor(name, shape, dt))
        ps = lambda name, shape: ctx.enter_context(nc.psum_tensor(name, shape, F32))
        sem = kp["sem"]
        w = sb("w_conv2", [128, 4 * C])
        prod = sb("w_products", [128, 4 * C])
        cov = sb("u_covariance", [128, C])
        mean_u = sb("u_mean", [128, 1])
        mean_row = sb("u_mean_row", [1, C])
        ones = sb("ones_column", [128, 1])
        t4 = sb("four_columns", [128, 6, 4])
        neg_gm = sb("neg_group_mean", [128, B])
        x_t = sb("x_tile", [128, XS, ROWS3 * W])
        u_t = sb("u_in", [128, US, UW])
        g_t = sb("gelu2_out", [128, GS, 4, UW])
        s_t = sb("pair_sums", [128, GS, 4, UW])
        junk = sb("junk3", [128, ROWS3 * W], BF16)
        cp = [ps(f"conv2_psum{i}", [128, 4, BANK]) for i in range(2)]

        s_w = sem("conv2_weights_loaded")
        s_lk = sem("vector_link3")
        s_v = sem("vector_result3")
        s_p = sem("tensor_result3")
        s_rs = sem("rstd_ready3")
        s_bn2 = sem("bn2_ready")
        s_x = [sem(f"x_in{i}") for i in range(XS)]
        s_u = [sem(f"u_in_loaded{i}") for i in range(US)]
        s_mm = sem("conv2_done")
        s_ge = sem("gelu2_done")
        s_bf = sem("pair_sums_done")
        s_half = sem("residual_added")
        s_y = sem("y_ready")
        s_sq = sem("y_squared")
        s_yst = [sem(f"y_stored{i}") for i in range(XS)]

        uv = u_d.rearrange("c b n -> b c n")
        xv = x.rearrange("b c h w -> b c (h w)")
        yv = y_d.rearrange("b c h w -> b c (h w)")
        XW = ROWS3 * W
        block = ctx.enter_context(nc.Block())

        @block.sync
        def _(sp):
            sp.dma_start(w[:], wc2).then_inc(s_w, 16)
            for i in range(XS):
                sp.sem_inc(s_yst[i], 16)
            with sp.Fori(0, B) as b:
                for k in range(UNITS3):
                    sp.wait_ge(s_sq, b * UNITS3 + k + 1)
                    sp.dma_start(u_t[:, k % US, :],
                                 uv[bass.ds(b, 1), :, k * UW:(k + 1) * UW].rearrange("b c n -> c (b n)")
                                 ).then_inc(s_u[k % US], 16)
                    sp.wait_ge(s_yst[k % XS], b * 16 * (UNITS3 // XS) + 16 * (k // XS + 1))
                    sp.dma_start(x_t[:, k % XS, :],
                                 xv[bass.ds(b, 1), :, k * XW:(k + 1) * XW].rearrange("b c n -> c (b n)")
                                 ).then_inc(s_x[k % XS], 16)

        @block.gpsimd
        def _(pool):
            pool.wait_ge(s_v, 5)
            nc.gpsimd.tensor_tensor(t4[:, 2, :], t4[:, 1, :], neg_half[:, 0:4], ALU.pow).then_inc(s_rs, 1)
            pool.sem_inc(s_bf, GS)
            with pool.Fori(0, B) as b:
                for k in range(UNITS3):
                    pool.wait_ge(s_ge, b * UNITS3 + k + 3)
                    pool.wait_ge(s_y, b * UNITS3 + k + 1)
                    gp = g_t[:, k % GS].rearrange("p (a b) n -> p a b n", b=2)
                    nc.gpsimd.tensor_tensor(s_t[:, k % GS, 0:2, :], gp[:, :, 0, :], gp[:, :, 1, :], ALU.add)
                    nc.gpsimd.tensor_tensor(s_t[:, k % GS, 2:4, :], gp[:, :, 0, :], gp[:, :, 1, :],
                                            ALU.subtract).then_inc(s_bf, 1)

        @block.vector
        def _(dve):
            N = float(B * HW2)
            lk = Chain(dve, s_lk)
            dve.sem_inc(s_y, GS)
            lk.link(nc.vector.memset(ones[:], 1.0))
            lk.link(nc.vector.tensor_scalar(neg_gm[:], kp["x_gmean"][:], -1.0, None, ALU.mult))
            nc.vector.tensor_scalar(mean_u[:], gram[:, C:C + 1], 1.0 / N, None, ALU.mult).then_inc(s_v, 1)
            dve.wait_ge(s_p, 1)
            nc.vector.tensor_copy(mean_row[:], cp[0][0:1, 0, 0:C]).then_inc(s_v, 1)
            dve.wait_ge(s_p, 2)
            nc.vector.scalar_tensor_tensor(cov[:], gram[:, 0:C], 1.0 / N, cp[0][:, 1, 0:C],
                                           ALU.mult, ALU.subtract).then_inc(s_v, 1)
            dve.wait_ge(s_p, 3)
            nc.vector.tensor_tensor(prod[:], w[:], cp[0][:, 2, :], ALU.mult).then_inc(s_v, 1)
            dve.wait_ge(s_p, 4)
            b2 = V[:, V_BC2:V_BC2 + 4]
            lk.link(nc.vector.tensor_tensor(t4[:, 0, :], cp[0][:, 3, 0:4], b2, ALU.add))
            nc.vector.tensor_scalar(t4[:, 1, :], cp[0][:, 3, 4:8], EPS, None, ALU.add).then_inc(s_v, 1)
            lk.link(nc.vector.tensor_tensor(t4[:, 3, :], b2, t4[:, 0, :], ALU.subtract))
            dve.wait_ge(s_rs, 1)
            lk.link(nc.vector.tensor_tensor(bn2_a[:], t4[:, 2, :], V[:, V_BN2G:V_BN2G + 4], ALU.mult))
            lk.link(nc.vector.tensor_tensor(t4[:, 4, :], t4[:, 3, :], bn2_a[:], ALU.mult))
            nc.vector.tensor_tensor(bn2_d[:], t4[:, 4, :], V[:, V_BN2B:V_BN2B + 4], ALU.add).then_inc(s_bn2, 1)
            with dve.Fori(0, B) as b:
                for k in range(UNITS3):
                    i = k % XS
                    dve.wait_ge(s_bf, b * UNITS3 + k + 1 + GS)
                    dve.wait_ge(s_x[i], b * 16 * (UNITS3 // XS) + 16 * (k // XS + 1))
                    xp = x_t[:, i, :].rearrange("c (i a j e) -> c a e i j", a=2, e=2, j=W2)
                    sums = s_t[:, k % GS].rearrange("c s (i j) -> c s i j", j=W2)
                    for a in range(2):
                        for e in range(2):
                            ins = nc.vector.scalar_tensor_tensor(xp[:, a, e], sums[:, 2 * a], 0.5, xp[:, a, e],
                                                                 ALU.mult, ALU.add)
                    ins.then_inc(s_half, 1)
                    dve.wait_ge(s_half, b * UNITS3 + k + 1)
                    for a in range(2):
                        for e in range(2):
                            ins = nc.vector.scalar_tensor_tensor(xp[:, a, e], sums[:, 2 * a + 1], (0.5, -0.5)[e],
                                                                 xp[:, a, e], ALU.mult, ALU.add)
                    ins.then_inc(s_y, 1)

        @block.tensor
        def _(pe):
            pe.wait_ge(s_w, 16)
            pe.wait_ge(s_v, 1)
            nc.tensor.matmul(cp[0][0:1, 0, 0:C], mean_u[:], K[:, K_ID:K_ID + C], start=True, stop=True).then_inc(s_p, 1)
            pe.wait_ge(s_v, 2)
            nc.tensor.matmul(cp[0][:, 1, 0:C], mean_row[:], mean_row[:], start=True, stop=True).then_inc(s_p, 1)
            pe.wait_ge(s_v, 3)
            nc.tensor.matmul(cp[0][:, 2, :], cov[:], w[:], start=True, stop=True).then_inc(s_p, 1)
            pe.wait_ge(s_v, 4)
            for s in range(4):
                nc.tensor.matmul(cp[0][:, 3, s:s + 1], w[:, s * C:(s + 1) * C], mean_u[:], start=True, stop=True)
                ins = nc.tensor.matmul(cp[0][:, 3, 4 + s:5 + s], prod[:, s * C:(s + 1) * C], ones[:], start=True, stop=True)
            ins.then_inc(s_p, 1)
            pe.wait_ge(s_bn2, 1)
            with pe.Fori(0, B) as b:
                for k in range(UNITS3):
                    pe.wait_ge(s_u[k % US], b * 16 * (UNITS3 // US) + 16 * (k // US + 1))
                    pe.wait_ge(s_ge, b * UNITS3 + k + 1)
                    for s in range(4):
                        ins = nc.tensor.matmul(cp[k % 2][:, s, :], w[:, s * C:(s + 1) * C], u_t[:, k % US, :],
                                               start=True, stop=True)
                    ins.then_inc(s_mm, 1)

        @block.scalar
        def _(act):
            act.sem_inc(s_ge, 2)
            act.sem_inc(s_sq, XS)
            act.wait_ge(s_bn2, 1)

            def finish(b, k):
                i = k % XS
                act.wait_ge(s_y, b * UNITS3 + k + 1 + GS)
                act.dma_start(yv[bass.ds(b, 1), :, k * XW:(k + 1) * XW].rearrange("b c n -> c (b n)"),
                              x_t[:, i, :]).then_inc(s_yst[i], 16)
                act.wait_ge(s_sq, b * UNITS3 + k + XS)
                nc.scalar.activation(junk[:], x_t[:, i, :], ACT.Square, bias=neg_gm[:, bass.ds(b, 1)],
                                     accum_out=kp["y_sq"][:, bass.ds(b, 1), k]).then_inc(s_sq, 1)

            def body(b, first):
                for k in range(UNITS3):
                    act.wait_ge(s_bf, b * UNITS3 + k + 1)
                    act.wait_ge(s_mm, b * UNITS3 + k + 1)
                    for s in range(4):
                        more = {"accum_out": kp["ll_sum"][:, bass.ds(b, 1), k]} if s == 0 else {}
                        ins = nc.scalar.activation(g_t[:, k % GS, s, :], cp[k % 2][:, s, :], ACT.Gelu,
                                                   scale=bn2_a[:, s:s + 1], bias=bn2_d[:, s:s + 1], **more)
                    ins.then_inc(s_ge, 1)
                    if k >= LAG_SQ:
                        finish(b, k - LAG_SQ)
                    elif not first:
                        finish(b - 1, UNITS3 + k - LAG_SQ)

            body(0, True)
            with act.Fori(1, B) as b:
                body(b, False)
            for k in range(UNITS3 - LAG_SQ, UNITS3):
                finish(B - 1, k)
            for i in range(XS):
                act.wait_ge(s_yst[i], 16 + 16 * B * UNITS3 // XS)


PADW = W + 4
BODY4 = 8
UNITS4 = B * NG
HCH = 16


def phase_blur(nc, kp, y_d, out):
    K, neg_half = kp["K"], kp["neg_half"]
    nm_b, rs_b = kp["nm_b"], kp["rs_b"]
    LAST = UNITS4 // BODY4 - 1
    with ExitStack() as ctx:
        sb = lambda name, shape, dt=F32: ctx.enter_context(nc.sbuf_tensor(name, shape, dt))
        ps = lambda name, shape: ctx.enter_context(nc.psum_tensor(name, shape, F32))
        sem = kp["sem"]
        band = sb("band", [128, 4, 128])
        band_hi = sb("band_hi", [128, 4, 128], F32R)
        band_lo = sb("band_lo", [128, 4, 128], F32R)
        cross = sb("cross", [128, 2, 128])
        cross_r = sb("cross_parts", [128, 2, 128], F32R)
        one_img = sb("ones_padded", [128, PADW])
        field = sb("blurred_ones", [128, 2, W])
        y_t = sb("y_tile", [128, 4, 2, GRP, W])
        y_hi = sb("y_hi", [128, 4, 2 * GRP, PADW], F32R)
        y_lo = sb("y_lo", [128, 4, 2 * GRP, PADW], F32R)
        halo = sb("halo", [HALO_P, 2, HCH, W])
        halo_r = sb("halo_parts", [HALO_P, 2, HCH, W], F32R)
        o_t = sb("out_tile", [128, 2, 2, GRP, W])
        st = sb("gn2_columns", [128, 8, B])
        spread = sb("gn2_spread", [128, 2, B, NG])
        rest_n = sb("rests_of_partition", [128, 1])
        rest_i = sb("rests", [1, 1], mybir.dt.int32)
        yp = [ps(f"blur_psum{i}", [128, GRP, W]) for i in range(4)]

        s_lk = sem("vector_link4")
        s_v = sem("vector_result4")
        s_p = sem("tensor_result4")
        s_rs = sem("rstd_ready4")
        s_set = sem("memsets_done4")
        s_ready = sem("blur_constants_ready")
        s_in = [sem(f"y_loaded{i}") for i in range(4)]
        s_hin = [sem(f"halo_loaded{i}") for i in range(2)]
        s_hhi = sem("halo_hi_ready")
        s_hlo = sem("halo_lo_ready")
        s_hi = sem("y_hi_ready")
        s_lo = sem("y_lo_ready")
        s_mm = sem("blur_half_done")
        s_ev = sem("blur_half_taken")
        s_o = sem("out_half_ready")
        s_st = [sem(f"out_stored{i}") for i in range(2)]

        yv = y_d.rearrange("b c h w -> (b c) h w")
        ov = out.rearrange("b c h w -> (b c) h w")
        block = ctx.enter_context(nc.Block())

        def load(sp, n, slot):
            for t in range(2):
                sp.dma_start(y_t[:, slot, t], yv[bass.ds(n * GRP, GRP), t * 128:(t + 1) * 128, :].rearrange(
                    "c p w -> p c w")).then_inc(s_in[slot], 16)

        def load_halo(sp, q, slot):
            for part in range(3):
                for kw in range(4):
                    lo, hi = max(0, 2 - kw), min(W, W + 2 - kw)
                    p0 = part * Q_STEP + kw * HALO_ROWS
                    sp.dma_start(halo[p0:p0 + HALO_ROWS, slot, :, lo:hi],
                                 yv[bass.ds(q * HCH, HCH), 126:126 + HALO_ROWS, lo + kw - 2:hi + kw - 2].rearrange(
                                     "c p w -> p c w")).then_inc(s_hin[slot], 16)

        @block.sync
        def _(sp):
            for n in range(4):
                load(sp, n, n)
            sp.wait_ge(s_set, 1)
            load_halo(sp, 0, 0)
            load_halo(sp, 1, 1)

            def body(it, last):
                for i in range(BODY4):
                    n = it * BODY4 + i
                    sp.wait_ge(s_o, n * 2 + 2)
                    for t in range(2):
                        sp.dma_start(ov[bass.ds(n * GRP, GRP), t * 128:(t + 1) * 128, :].rearrange("c p w -> p c w"),
                                     o_t[:, i % 2, t]).then_inc(s_st[i % 2], 16)
                    if not (last and i >= 4):
                        load(sp, n + 4, i % 4)
                    if i % 4 == 1 and not last:
                        sp.wait_ge(s_hlo, it * 2 + i // 4 + 1)
                        load_halo(sp, it * 2 + i // 4 + 2, i // 4)

            with sp.Fori(0, LAST) as it:
                body(it, False)
            body(LAST, True)
            for i in range(2):
                sp.wait_ge(s_st[i], 32 + 32 * UNITS4 // 2)

        @block.gpsimd
        def _(pool):
            pool.memset(halo[:], 0.0).then_inc(s_set, 1)
            pool.memset(one_img[:], 0.0).then_inc(s_set, 1)
            for y in (y_hi, y_lo):
                for cols in (slice(0, 2), slice(2 + W, PADW)):
                    pool.memset(y[:, :, :, cols].bitcast(F32), 0.0).then_inc(s_set, 1)
            pool.wait_ge(s_set, 6)
            pool.memset(one_img[:, 2:2 + W], 1.0).then_inc(s_set, 1)
            pool.wait_ge(s_v, 3)
            nc.gpsimd.tensor_tensor(st[:, 6, :], st[:, 5, :], neg_half[:, 0:B], ALU.pow).then_inc(s_rs, 1)

            def body(it, last):
                for i in range(BODY4):
                    pool.wait_ge(s_hi, it * BODY4 + i + 1)
                    nc.gpsimd.tensor_tensor(
                        y_lo[:, i % 4, :, 2:2 + W], y_t[:, i % 4].rearrange("p t c w -> p (t c) w"),
                        y_hi[:, i % 4, :, 2:2 + W].bitcast(F32), ALU.subtract).then_inc(s_lo, 1)

            with pool.Fori(0, LAST) as it:
                body(it, False)
            body(LAST, True)

        @block.scalar
        def _(act):
            def split_halo(loaded, slot):
                act.wait_ge(s_hin[slot], loaded)
                nc.scalar.activation(halo_r[:, slot], halo[:, slot], ACT.Copy).then_inc(s_hhi, 1)

            split_halo(12 * 16, 0)

            def body(it, last):
                for i in range(BODY4):
                    n = it * BODY4 + i
                    act.wait_ge(s_in[i % 4], it * 64 + 32 * (i // 4 + 1))
                    act.wait_ge(s_mm, n * 2 + 2)
                    nc.scalar.activation(y_hi[:, i % 4, :, 2:2 + W], y_t[:, i % 4].rearrange("p t c w -> p (t c) w"),
                                         ACT.Copy).then_inc(s_hi, 1)
                    if i % 4 == 3 and not (last and i > 4):
                        nxt = i // 4 + 1
                        split_halo((it + nxt // 2 + 1) * (12 * 16), nxt % 2)

            with act.Fori(0, LAST) as it:
                body(it, False)
            body(LAST, True)

        @block.vector
        def _(dve):
            lk = Chain(dve, s_lk)
            NCH = float(HW)
            lk.link(nc.vector.reduce_sum(st[:, 0, :], kp["ll_sum"][:], AX.X))
            lk.link(nc.vector.tensor_tensor(st[:, 1, :], kp["x_cmean"][:], kp["x_gmean"][:], ALU.subtract))
            lk.link(nc.vector.scalar_tensor_tensor(st[:, 2, :], st[:, 0, :], 2.0 / NCH, st[:, 1, :], ALU.mult, ALU.add))
            lk.link(nc.vector.reduce_sum(st[:, 4, :], kp["y_sq"][:], AX.X))
            nc.vector.tensor_scalar(st[:, 3, :], st[:, 4, :], 1.0 / NCH, None, ALU.mult).then_inc(s_v, 2)
            for kw in range(4):
                for kh in range(4):
                    mask = K[:, K_TM + kh * 128:K_TM + (kh + 1) * 128]
                    scalar = kp["KR"][:, kh * 4 + kw:kh * 4 + kw + 1]
                    if kh == 0:
                        lk.link(nc.vector.tensor_scalar(band[:, kw, :], mask, scalar, None, ALU.mult))
                    else:
                        lk.link(nc.vector.scalar_tensor_tensor(band[:, kw, :], mask, scalar, band[:, kw, :],
                                                               ALU.mult, ALU.add))
            for t in range(2):
                for kh in range(4):
                    mask = K[:, K_HM + (t * 4 + kh) * 128:K_HM + (t * 4 + kh + 1) * 128]
                    scalar = kp["HK"][:, kh:kh + 1]
                    if kh == 0:
                        lk.link(nc.vector.tensor_scalar(cross[:, t, :], mask, scalar, None, ALU.mult))
                    else:
                        lk.link(nc.vector.scalar_tensor_tensor(cross[:, t, :], mask, scalar, cross[:, t, :],
                                                               ALU.mult, ALU.add))
            lk.link(nc.vector.tensor_copy(band_hi[:], band[:]))
            lk.link(nc.vector.tensor_tensor(band_lo[:], band[:], band_hi[:].bitcast(F32), ALU.subtract))
            dve.wait_ge(s_p, 1)
            small = yp[0][:].rearrange("p c w -> p (c w)")
            lk.link(nc.vector.tensor_copy(st[:, 4, :], small[:, 0:B]))
            lk.link(nc.vector.tensor_tensor(st[:, 7, :], st[:, 4, :], st[:, 4, :], ALU.mult))
            lk.link(nc.vector.tensor_tensor(st[:, 5, :], small[:, B:2 * B], st[:, 7, :], ALU.subtract))
            nc.vector.tensor_scalar(st[:, 5, :], st[:, 5, :], EPS, None, ALU.add).then_inc(s_v, 1)
            lk.link(nc.vector.tensor_tensor(st[:, 7, :], st[:, 4, :], kp["x_gmean"][:], ALU.add))
            lk.link(nc.vector.tensor_scalar(st[:, 7, :], st[:, 7, :], -1.0, None, ALU.mult))
            dve.wait_ge(s_rs, 1)
            for b in range(B):
                for j, col in enumerate((7, 6)):
                    ins = nc.vector.tensor_scalar(spread[:, j, b, :], K[:, K_GM:K_GM + NG], st[:, col, b:b + 1],
                                                  None, ALU.mult)
            ins.then_inc(s_v, 1)
            dve.wait_ge(s_p, 2)
            lk.link(nc.vector.tensor_copy(nm_b[:].rearrange("p b g -> p (b g)"), small[:, 512:512 + B * NG]))
            lk.link(nc.vector.tensor_copy(rs_b[:].rearrange("p b g -> p (b g)"), small[:, 512 + B * NG:512 + 2 * B * NG]))
            lk.link(nc.vector.tensor_scalar(o_t[:, 0, 0, 0:2, :].rearrange("p c w -> p (c w)"),
                                            band_lo[:].bitcast(F32).rearrange("p k m -> p (k m)"), 0.0, None, ALU.not_equal, ALU.add,
                                            accum_out=rest_n[:]))
            lk.link(nc.vector.tensor_copy(cross_r[:], cross[:]))
            third = slice(2 * Q_STEP, 3 * Q_STEP)
            nc.vector.tensor_tensor(cross_r[third], cross[third], cross_r[third].bitcast(F32),
                                    ALU.subtract).then_inc(s_v, 1)
            dve.wait_ge(s_p, 3)
            lk.link(nc.vector.tensor_copy(rest_i[:], yp[3][0:1, 0, 0:1]))
            for t in range(2):
                ins = nc.vector.tensor_copy(field[:, t, :], yp[1 + t][:, 0, :])
            ins.then_inc(s_ready, 1)
            dve.wait_ge(s_ready, 1)
            for i in range(2):
                dve.sem_inc(s_st[i], 32)

            def halo_rest(q, slot):
                part = slice(Q_STEP, Q_STEP + 4 * HALO_ROWS)
                dve.wait_ge(s_hhi, q + 1)
                nc.vector.tensor_tensor(halo_r[part, slot], halo[part, slot], halo_r[part, slot].bitcast(F32),
                                        ALU.subtract).then_inc(s_hlo, 1)

            halo_rest(0, 0)

            def body(it, last):
                for i in range(BODY4):
                    n = it * BODY4 + i
                    col = n
                    if i % 4 == 3 and not (last and i > 4):
                        halo_rest(it * 2 + i // 4 + 1, (i // 4 + 1) % 2)
                    for t in range(2):
                        dve.wait_ge(s_mm, n * 2 + t + 9)
                        if t == 0:
                            dve.wait_ge(s_st[i % 2], it * (32 * BODY4 // 2) + 32 * (i // 2 + 1))
                        res = o_t[:, i % 2, t]
                        nc.vector.scalar_tensor_tensor(
                            res, field[:, t:t + 1, :].to_broadcast([128, GRP, W]),
                            nm_b[:].rearrange("p b g -> p (b g)")[:, bass.ds(col, 1)],
                            yp[2 * (i % 2) + t][:], ALU.mult, ALU.add).then_inc(s_ev, 1)
                        dve.wait_ge(s_ev, n * 2 + t + 5)
                        nc.vector.scalar_tensor_tensor(
                            res, res, rs_b[:].rearrange("p b g -> p (b g)")[:, bass.ds(col, 1)],
                            y_t[:, i % 4, t], ALU.mult, ALU.add).then_inc(s_o, 1)

            with dve.Fori(0, LAST) as it:
                body(it, False)
            body(LAST, True)

        @block.tensor
        def _(pe):
            pe.sem_inc(s_mm, 8)
            small = yp[0][:].rearrange("p c w -> p (c w)")
            pe.wait_ge(s_v, 2)
            nc.tensor.matmul(small[:, 0:2 * B], K[:, K_G4:K_G4 + C], st[:, 2:4, :].rearrange("p a b -> p (a b)"),
                             start=True, stop=True).then_inc(s_p, 1)
            pe.wait_ge(s_v, 4)
            nc.tensor.matmul(small[:, 512:512 + 2 * B * NG], kp["quarter"][:], spread[:].rearrange("p j b g -> p (j b g)"),
                             start=True, stop=True).then_inc(s_p, 1)
            pe.wait_ge(s_v, 5)
            pe.wait_ge(s_set, 7)
            for t in range(2):
                for kw in range(4):
                    nc.tensor.matmul(yp[1 + t][:, 0, :], band[:, kw, :], one_img[:, kw:kw + W],
                                     start=(kw == 0), stop=False)
                ins = nc.tensor.matmul(yp[1 + t][:, 0, :], cross[0:4 * HALO_ROWS, t, :],
                                       K[0:4 * HALO_ROWS, K_H1:K_H1 + W], start=False, stop=True)
            nc.tensor.matmul(yp[3][0:1, 0, 0:1], rest_n[:], one_img[:, 2:3], start=True, stop=True).then_inc(s_p, 1)
            pe.sem_inc(s_ev, 4)
            pe.wait_ge(s_ready, 1)


            def body(it, products):
                for i in range(BODY4):
                    n = it * BODY4 + i
                    pe.wait_ge(s_lo, n + 1)
                    if i % 4 == 0:
                        pe.wait_ge(s_hlo, it * 2 + i // 4 + 1)
                    for t in range(2):
                        pe.wait_ge(s_ev, n * 2 + t + 1)
                        dst = [yp[2 * (i % 2) + t][:, 2 * c:2 * c + 2, :] for c in range(2)]
                        src = lambda y, c, kw: y[:, i % 4, t * GRP + 2 * c:t * GRP + 2 * c + 2, kw:kw + W]
                        for kw in range(4):
                            for m, (wt, y) in enumerate(products):
                                for c in range(2):
                                    nc.tensor.matmul(dst[c], wt[:, kw, :], src(y, c, kw),
                                                     start=(kw == 0 and m == 0), stop=False)
                        for c in range(2):
                            ch = (i % 4) * GRP + 2 * c
                            ins = nc.tensor.matmul(dst[c], cross_r[0:HALO_P, t, :],
                                                   halo_r[:, i // 4, ch:ch + 2, :], start=False, stop=True)
                        ins.then_inc(s_mm, 1)

            rests = pe.value_load(rest_i[0:1, 0:1], min_val=0, max_val=4 * 128 * 128)
            with pe.If(rests == 0):
                with pe.Fori(0, LAST + 1) as it:
                    body(it, ((band_hi, y_hi), (band_hi, y_lo)))
            with pe.Else():
                with pe.Fori(0, LAST + 1) as it:
                    body(it, ((band_hi, y_hi), (band_hi, y_lo), (band_lo, y_hi)))


def kernel(x, L0_conv_w_c1, L0_conv_b_c1, L0_conv_bn1_g, L0_conv_bn1_b, L0_conv_dw_w, L0_conv_dw_b,
           L0_conv_gn_g, L0_conv_gn_b, L0_conv_pw1_w, L0_conv_pw1_b, L0_conv_pw2_w, L0_conv_pw2_b,
           L0_conv_w_c2, L0_conv_b_c2, L0_conv_bn2_g, L0_conv_bn2_b, L1_conv_kernel):
    import concourse.bacc as bacc
    from concourse.bass_utils import run_bass_kernel_spmd

    def a(v):
        return np.asarray(v)

    def halo_taps():
        taps = a(L1_conv_kernel)[::-1, ::-1]
        rows = np.zeros((128, 4), np.float32)
        for q in range(3):
            for kw in range(4):
                for r in range(HALO_ROWS):
                    rows[q * Q_STEP + kw * HALO_ROWS + r] = taps[:, kw]
        return rows

    vec = np.concatenate(
        [np.stack([a(v) for v in (L0_conv_b_c1, L0_conv_bn1_g, L0_conv_bn1_b, L0_conv_dw_b, L0_conv_gn_g,
                                  L0_conv_gn_b, L0_conv_pw1_b, L0_conv_pw2_b)], axis=1)]
        + [a(v).reshape(4, C).T for v in (L0_conv_b_c2, L0_conv_bn2_g, L0_conv_bn2_b)]
        + [a(L0_conv_dw_w).reshape(C, TAPS)], axis=1)
    arrays = {
        "x": a(x),
        "vec": vec,
        "wc1": a(L0_conv_w_c1).reshape(C, 4, C).transpose(2, 1, 0),
        "pw1": a(L0_conv_pw1_w).T,
        "pw2": a(L0_conv_pw2_w).T,
        "wc2": a(L0_conv_w_c2).T,
        "kern": np.broadcast_to(a(L1_conv_kernel)[::-1, ::-1].reshape(1, 16), (128, 16)),
        "halo_k": halo_taps(),
        "const": shape_constants(),
    }
    arrays = {k: np.ascontiguousarray(v) for k, v in arrays.items()}
    nc = bacc.Bacc("TRN2", target_bir_lowering=False, num_devices=1)
    args = [nc.dram_tensor(k, v.shape, mybir.dt.from_np(v.dtype), kind="ExternalInput").ap()
            for k, v in arrays.items()]
    out = nc.dram_tensor("out", (B, C, H, W), F32, kind="ExternalOutput").ap()
    build(nc, *args, out)
    r = run_bass_kernel_spmd(nc, [arrays], core_ids=[0])
    return r.results[0]["out"]
```
